# Optimizing a Trainium2 kernel written in Bass

```python
import numpy as np
import jax
import jax.numpy as jnp

def _softmax(x, axis=-1):
    return jax.nn.softmax(x, axis=axis)

def _gelu(x):
    return jax.nn.gelu(x, approximate=True)

def _silu(x):
    return jax.nn.silu(x)

def _sigmoid(x):
    return jax.nn.sigmoid(x)

def _layernorm(x, axis=-1, eps=1e-05):
    m = jnp.mean(x, axis=axis, keepdims=True)
    v = jnp.var(x, axis=axis, keepdims=True)
    return (x - m) / jnp.sqrt(v + eps)

def _scatter_add(tgt, idx, src, axis=0):
    return tgt.at[idx].add(src)

def _segment_sum(src, seg, n):
    return jax.ops.segment_sum(src, seg, n)
kernel_name = 'mk_xattn_ffn_d1_seqx_r8_46d296'

def setup_inputs(seed: int=0):
    np.random.seed(seed)
    _w = jnp.asarray

    def _rec_inputs():
        import jax
        import jax.numpy as jnp
        _rk = jax.random.key(seed)
        x = -0.0003929 + 0.9999 * jax.random.normal(jax.random.fold_in(_rk, 1), (4, 256, 128), jnp.float32)
        _lenS = 256 - jax.random.randint(jax.random.fold_in(_rk, 7), (4,), 0, max(1, 256 // 4) + 1, jnp.int32)
        _lenS2 = 1601 - jax.random.randint(jax.random.fold_in(_rk, 8), (4,), 0, max(1, 1601 // 4) + 1, jnp.int32)
        _ctx_1024P = jax.random.normal(jax.random.fold_in(_rk, 11), (4, 16, 128), jnp.float32)
        _ctx_1024c = jax.random.dirichlet(jax.random.fold_in(_rk, 511), 0.3 * jnp.ones((16,), jnp.float32), (4, 1601))
        _ctx_1024t = jnp.einsum('bsk,bkd->bsd', _ctx_1024c, _ctx_1024P)
        _ctx_1024t = _ctx_1024t * jax.lax.rsqrt(jnp.mean(jnp.square(_ctx_1024t)) + 1e-12) * 0.953939
        ctx_1024 = 2.81802e-05 + 1.00001 * (_ctx_1024t + 0.3 * jax.random.normal(jax.random.fold_in(_rk, 611), (4, 1601, 128), jnp.float32))
        return (x, ctx_1024)
    x, ctx_1024 = _rec_inputs()

    def _L0_xattn_setup():
        import jax, jax.numpy as jnp
        import numpy as np
        IN_CH = 128
        ATT_DIM = 128
        B, L1, L2 = (8, 256, 256)
        key = jax.random.key(seed)
        ks = jax.random.split(key, 8)
        s = 1.0 / np.sqrt(IN_CH)
        return {'input_1': jax.random.normal(ks[0], (B, L1, IN_CH), dtype=jnp.float32), 'input_2': jax.random.normal(ks[1], (B, L2, IN_CH), dtype=jnp.float32), 'Wq': jax.random.uniform(ks[2], (IN_CH, ATT_DIM), jnp.float32, -s, s), 'bq': jnp.zeros((ATT_DIM,), jnp.float32), 'Wk': jax.random.uniform(ks[3], (IN_CH, ATT_DIM), jnp.float32, -s, s), 'bk': jnp.zeros((ATT_DIM,), jnp.float32), 'Wv': jax.random.uniform(ks[4], (IN_CH, ATT_DIM), jnp.float32, -s, s), 'bv': jnp.zeros((ATT_DIM,), jnp.float32)}
    _L0_xattn_all = _L0_xattn_setup()
    _L0_xattn_in = {k: v for k, v in _L0_xattn_all.items() if k in ('Wq', 'bq', 'Wk', 'bk', 'Wv', 'bv')}
    del _L0_xattn_all

    def _L0_ffn_setup():
        import jax, jax.numpy as jnp
        import numpy as np
        ALPHA = 1.702
        LIMIT = 7.0
        TOP_K = 2
        key = jax.random.key(seed)
        ks = jax.random.split(key, 4)
        B, S, H, E, I = (2, 128, 128, 8, 256)
        return {'hidden_states': jax.random.normal(ks[0], (B, S, H), jnp.float32), 'router_weight': jax.random.normal(ks[1], (E, H), jnp.float32), 'router_bias': jnp.zeros((E,), jnp.float32), 'gate_up_proj': jax.random.normal(ks[2], (E, H, 2 * I), jnp.float32) * 0.02, 'gate_up_bias': jnp.zeros((E, 2 * I), jnp.float32), 'down_proj': jax.random.normal(ks[3], (E, I, H), jnp.float32) * 0.02, 'down_bias': jnp.zeros((E, H), jnp.float32)}
    _L0_ffn_all = _L0_ffn_setup()
    _L0_ffn_in = {k: v for k, v in _L0_ffn_all.items() if k in ('router_weight', 'router_bias', 'gate_up_proj', 'gate_up_bias', 'down_proj', 'down_bias')}
    del _L0_ffn_all
    return {'x': x, 'ctx_1024': ctx_1024, 'L0_xattn_Wq': _L0_xattn_in['Wq'], 'L0_xattn_bq': _L0_xattn_in['bq'], 'L0_xattn_Wk': _L0_xattn_in['Wk'], 'L0_xattn_bk': _L0_xattn_in['bk'], 'L0_xattn_Wv': _L0_xattn_in['Wv'], 'L0_xattn_bv': _L0_xattn_in['bv'], 'L0_ffn_router_weight': _L0_ffn_in['router_weight'], 'L0_ffn_router_bias': _L0_ffn_in['router_bias'], 'L0_ffn_gate_up_proj': _L0_ffn_in['gate_up_proj'], 'L0_ffn_gate_up_bias': _L0_ffn_in['gate_up_bias'], 'L0_ffn_down_proj': _L0_ffn_in['down_proj'], 'L0_ffn_down_bias': _L0_ffn_in['down_bias']}

def reference(x, ctx_1024, L0_xattn_Wq, L0_xattn_bq, L0_xattn_Wk, L0_xattn_bk, L0_xattn_Wv, L0_xattn_bv, L0_ffn_router_weight, L0_ffn_router_bias, L0_ffn_gate_up_proj, L0_ffn_gate_up_bias, L0_ffn_down_proj, L0_ffn_down_bias):
    import jax
    import jax.numpy as jnp

    def _L0_xattn_ref(input_1, input_2, Wq, bq, Wk, bk, Wv, bv):
        import jax, jax.numpy as jnp
        import numpy as np
        IN_CH = 128
        ATT_DIM = 128
        B, L1, L2 = (8, 256, 256)
        scale = 1.0 / np.sqrt(ATT_DIM).astype(np.float32)
        Q = jnp.einsum('bld,de->ble', input_1, Wq) + bq
        K = jnp.einsum('bld,de->ble', input_2, Wk) + bk
        V = jnp.einsum('bld,de->ble', input_2, Wv) + bv
        scores = jnp.einsum('bqd,bkd->bqk', Q, K) * scale
        scores = jnp.clip(scores, -100.0, 100.0)
        weights = jax.nn.softmax(scores, axis=-1)
        return jnp.einsum('bqk,bkd->bqd', weights, V)

    def _L0_ffn_ref(hidden_states, router_weight, router_bias, gate_up_proj, gate_up_bias, down_proj, down_bias):
        import jax, jax.numpy as jnp
        import numpy as np
        ALPHA = 1.702
        LIMIT = 7.0
        TOP_K = 2
        B, S, H = hidden_states.shape
        E, _, two_I = gate_up_proj.shape
        I = two_I // 2
        flat = hidden_states.reshape(B * S, H)
        logits = flat @ router_weight.T + router_bias
        scores = jax.nn.softmax(logits, axis=-1)
        topk_w, topk_idx = jax.lax.top_k(scores, TOP_K)
        gu = jnp.einsum('th,ehn->ten', flat, gate_up_proj) + gate_up_bias
        gate = jnp.minimum(gu[..., :I], LIMIT)
        up = jnp.clip(gu[..., I:], -LIMIT, LIMIT)
        glu = gate * jax.nn.sigmoid(gate * ALPHA)
        act = (up + 1.0) * glu
        down = jnp.einsum('tei,eih->teh', act, down_proj) + down_bias
        gathered = jnp.take_along_axis(down, topk_idx[:, :, None], axis=1)
        out = (gathered * topk_w[:, :, None]).sum(axis=1)
        return out.reshape(B, S, H)
    x = x + _L0_xattn_ref(_layernorm(x, axis=-1), ctx_1024, L0_xattn_Wq, L0_xattn_bq, L0_xattn_Wk, L0_xattn_bk, L0_xattn_Wv, L0_xattn_bv)
    x = x + _L0_ffn_ref(_layernorm(x, axis=-1), L0_ffn_router_weight, L0_ffn_router_bias, L0_ffn_gate_up_proj, L0_ffn_gate_up_bias, L0_ffn_down_proj, L0_ffn_down_bias)
    return x

_drawn_inputs = setup_inputs


def setup_inputs(seed=0):
    import zlib

    import numpy as np

    out = dict(_drawn_inputs(seed))
    spreads = {'L0_xattn_bq': (0.0, 0.8),
     'L0_xattn_bk': (0.0, 2.0),
     'L0_xattn_bv': (0.0, 0.1),
     'L0_ffn_router_bias': (0.0, 2.0),
     'L0_ffn_gate_up_bias': (0.0, 0.512),
     'L0_ffn_down_bias': (0.0, 0.1)}
    factors = {}
    for name, (base, spread) in spreads.items():
        noise = np.random.default_rng([zlib.crc32(name.encode()), seed]).standard_normal(out[name].shape)
        drawn = base * np.exp(spread * noise) if base else spread * noise
        out[name] = jnp.asarray(drawn.astype(out[name].dtype))
    for name, factor in factors.items():
        out[name] = (out[name] * factor).astype(out[name].dtype)
    return out
```

```python
import numpy as np
import concourse.bass as bass
from concourse import mybir
from contextlib import ExitStack

F32 = mybir.dt.float32
F32R = mybir.dt.float32r
ALU = mybir.AluOpType
ACT = mybir.ActivationFunctionType
AX = mybir.AxisListType

BATCHES, QUERIES, DIM = 4, 256, 128
KEYS = 1601
EXPERTS, HIDDEN, TOP_K = 8, 256, 2
P = 128
TILES = BATCHES * QUERIES // P
TPB = QUERIES // P
KT_FULL = KEYS // P
KT = KT_FULL + 1
K_REST = KEYS - KT_FULL * P
KEYS_EVEN = KEYS + KEYS % 2
SCALE = float(1.0 / np.sqrt(DIM).astype(np.float32))
CLIP = 100.0
EPS = 1e-5
ALPHA, LIMIT = 1.702, 7.0
E_BASE = float(np.float32(np.e))

_CW = KEYS // 4 // 2 * 2
SCORE_CHUNKS = [(c * _CW, _CW, _CW) for c in range(3)] + [(3 * _CW, KEYS - 3 * _CW, KEYS_EVEN - 3 * _CW)]
NCH = len(SCORE_CHUNKS)
PREP = [(0, 2), (2, 3), (5, 3)]
CTX_GROUPS = [(t, min(4, KT - t)) for t in range(0, KT, 4)]
PT_GROUPS = [(t, min(2, KT - t)) for t in range(0, KT, 2)]
PAIRS = EXPERTS // 2
HALF = TILES // 2
HTOK = HALF * P
STEPS = 2 * EXPERTS
PAIR_STEPS = [(0, 0), (1, 0), (0, 1), (1, 1)]


def _transpose_bank_uses():
    order = [("ctx", 0, g) for g in range(len(CTX_GROUPS))]
    for b in range(BATCHES):
        if b + 1 < BATCHES:
            order += [("ctx", b + 1, g) for g in range(len(CTX_GROUPS))]
        if b >= 1:
            order += [("pt", b - 1, g) for g in range(len(PT_GROUPS))]
    order += [("pt", BATCHES - 1, g) for g in range(len(PT_GROUPS))]
    seen, found = [0, 0], {}
    for kind, b, g in order:
        found[kind, b, g] = (g % 2, seen[g % 2])
        seen[g % 2] += 1
    return found, seen


T_USE, T_TOTAL = _transpose_bank_uses()


def build(nc, x, ctx_in, wq, wkT, bqk, wv, bv, wrT, rb, gu, gub, dn, db, out):
    es = ExitStack()
    with es:
        def sb(name, shape, dt=F32):
            return es.enter_context(nc.sbuf_tensor(name, shape, dt))

        def sem(name):
            return es.enter_context(nc.semaphore(name))

        x_sb = sb("x_sb", [P, TILES, DIM])
        ctx_sb = [sb(f"ctx_sb{b}", [P, KT, DIM]) for b in range(BATCHES)]
        wq_sb = sb("wq_sb", [P, DIM])
        wkT_sb = sb("wkT_sb", [P, DIM])
        bqk_sb = sb("bqk_sb", [P, 2])
        wv_sb = sb("wv_sb", [P, DIM])
        bv_sb = sb("bv_sb", [P, DIM])
        wr_sb = sb("wr_sb", [P, EXPERTS])
        rb_sb = sb("rb_sb", [P, EXPERTS])
        gu_sb = sb("gu_sb", [P, EXPERTS * 2 * HIDDEN])
        gub_sb = sb("gub_sb", [P, EXPERTS * 4])
        gub1_sb = sb("gub1_sb", [P, EXPERTS * 4])
        dn_sb = sb("dn_sb", [P, EXPERTS * 2 * DIM])
        db_sb = sb("db_sb", [EXPERTS, DIM])
        ident = sb("ident", [P, P])
        before = sb("before", [P, EXPERTS, EXPERTS])
        minus_half = sb("minus_half", [P, TILES])
        e_base = sb("e_base", [P, HALF * EXPERTS])
        stats = sb("stats", [P, TILES, 6])
        mv = sb("mv", [P, TILES, 2])
        ve = sb("ve", [P, TILES])
        rstd = sb("rstd", [P, TILES])
        xn = sb("xn", [P, TILES, DIM])
        stats2 = sb("stats2", [P, TILES, 6])
        mv2 = sb("mv2", [P, TILES, 2])
        ve2 = sb("ve2", [P, TILES])
        rstd2 = sb("rstd2", [P, TILES])
        xn2 = sb("xn2", [P, TILES, DIM])
        xT = sb("xT", [P, TILES * P])
        qT = sb("qT", [P, TILES * P])
        g_hi = sb("g_hi", [P, TILES * P], F32R)
        g_lo = sb("g_lo", [P, TILES * P], F32R)
        clip_hi = sb("clip_hi", [P, TILES])
        row_max = sb("row_max", [P, TILES, NCH + 1])
        neg_max = sb("neg_max", [P, TILES])
        row_sum = sb("row_sum", [P, TILES])
        inv_sum = sb("inv_sum", [P, TILES])
        ct_hi = [sb(f"ct_hi{i}", [P, KEYS_EVEN], F32R) for i in range(2)]
        ct_lo = [sb(f"ct_lo{i}", [P, KEYS_EVEN], F32R) for i in range(2)]
        sc = sb("sc", [P, TPB, KEYS_EVEN])
        pr = sb("pr", [P, 2, TPB, KEYS_EVEN])
        pT = sb("pT", [P, KT, TPB * P])
        oT = sb("oT", [P, TPB * P])
        xb = sb("xb", [P, TILES, DIM])
        x1 = sb("x1", [P, TILES, DIM])
        x2_hi = sb("x2_hi", [P, TILES * P], F32R)
        x2_lo = sb("x2_lo", [P, TILES * P], F32R)
        wr_hi = sb("wr_hi", [P, EXPERTS], F32R)
        wr_lo = sb("wr_lo", [P, EXPERTS], F32R)
        logit = sb("logit", [P, TILES, EXPERTS])
        lmax = sb("lmax", [P, TILES])
        ex = sb("ex", [P, TILES, EXPERTS])
        esum = sb("esum", [P, TILES])
        prob = sb("prob", [P, TILES, EXPERTS])
        beats = sb("beats", [P, HALF * EXPERTS, EXPERTS])
        ties = sb("ties", [P, HALF * EXPERTS, EXPERTS])
        rank = sb("rank", [P, TILES, EXPERTS])
        w_route = sb("w_route", [P, TILES, EXPERTS])
        w_scaled = sb("w_scaled", [P, TILES * EXPERTS])
        wT = sb("wT", [EXPERTS, TILES * P])
        w_hi = [sb(f"w_hi{i}", [P, 2 * HIDDEN], F32R) for i in range(2)]
        w_lo = [sb(f"w_lo{i}", [P, 2 * HIDDEN], F32R) for i in range(2)]
        gate = sb("gate", [P, 2, 2, HTOK])
        up = sb("up", [P, 2, 2, HTOK])
        act_t = [old[:].rearrange("p (c t) -> p c t", c=2) for old in (xT, qT)]
        y_sb = xn2[:].rearrange("p (k t) d -> p k (t d)", k=2)
        out_sb = xn

        S = [es.enter_context(nc.psum_tensor(f"S{i}", [P, 512], F32)) for i in range(4)]
        T = [es.enter_context(nc.psum_tensor(f"T{i}", [P, 512], F32)) for i in range(2)]
        O = es.enter_context(nc.psum_tensor("O", [P, 512], F32))
        M = es.enter_context(nc.psum_tensor("M", [P, 512], F32))

        x0_in, x1_in, qk_in, route_in = sem("x0_in"), sem("x1_in"), sem("qk_in"), sem("route_in")
        ctx_in_s = [sem(f"ctx_in{b}") for b in range(BATCHES)]
        v_in, gu_in, dn_in, out_done = sem("v_in"), sem("gu_in"), sem("dn_in"), sem("out_done")
        const_ready = sem("const_ready")
        pad_ready = sem("pad_ready")
        var_ready, rstd_ready, xn_ready = sem("var_ready"), sem("rstd_ready"), sem("xn_ready")
        var2_ready, rstd2_ready, xn2_ready = sem("var2_ready"), sem("rstd2_ready"), sem("xn2_ready")
        xT_done, xT_copied, q_done, q_copied = sem("xT_done"), sem("xT_copied"), sem("q_done"), sem("q_copied")
        g_done, g_hi_ready, g_lo_ready, clip_ready = sem("g_done"), sem("g_hi_ready"), sem("g_lo_ready"), sem("clip_ready")
        t_done, t_free = [sem("t_done0"), sem("t_done1")], [sem("t_free0"), sem("t_free1")]
        ct_hi_ready = sem("ct_hi_ready")
        s_done, s_free = sem("s_done"), sem("s_free")
        negmax_ready, clipped, p_ready = sem("negmax_ready"), sem("clipped"), sem("p_ready")
        o_done, oT_copied, v_done, x1_ready = sem("o_done"), sem("oT_copied"), sem("v_done"), sem("x1_ready")
        xb_ready, inv_ready = sem("xb_ready"), sem("inv_ready")
        x2_done, x2_hi_ready, x2_lo_ready = sem("x2_done"), sem("x2_hi_ready"), sem("x2_lo_ready")
        r_done, logit_ready, ldiff_ready, exp_ready = sem("r_done"), sem("logit_ready"), sem("ldiff_ready"), sem("exp_ready")
        route_ready = sem("route_ready")
        chain = sem("chain")
        w_ready = sem("w_ready")
        w_hi_ready = sem("w_hi_ready")
        gub1_ready = sem("gub1_ready")
        gu_done, gate_copied, up_copied = sem("gu_done"), sem("gate_copied"), sem("up_copied")
        silu_ready, up_clipped, act_ready = sem("silu_ready"), sem("up_clipped"), sem("act_ready")
        y_done, y_scaled, y_added = sem("y_done"), sem("y_scaled"), sem("y_added")
        wT_done, wT_copied, db_done, out_ready = sem("wT_done"), sem("wT_copied"), sem("db_done"), sem("out_ready")

        block = es.enter_context(nc.Block())

        x_v = x.rearrange("b (t p) d -> p (b t) d", p=P)
        out_v = out.rearrange("b (t p) d -> p (b t) d", p=P)
        SETUP_CONSTS = 6

        @block.sync
        def _(sp):
            sp.dma_start(x_sb[:, 0:TPB], x_v[:, 0:TPB]).then_inc(x0_in, 16)
            for b in range(BATCHES):
                sp.dma_start(ctx_sb[b][:, 0:KT_FULL, :],
                             ctx_in[b, 0:KT_FULL * P, :].rearrange("(p t) d -> p t d", t=KT_FULL)).then_inc(ctx_in_s[b], 16)
                sp.dma_start(ctx_sb[b][0:K_REST, KT_FULL, :], ctx_in[b, KT_FULL * P:KEYS, :]).then_inc(ctx_in_s[b], 16)
                if b == 0:
                    sp.dma_start(x_sb[:, TPB:TILES], x_v[:, TPB:TILES]).then_inc(x1_in, 16)
            sp.dma_start(gu_sb[:].rearrange("p (e n) -> p e n", e=EXPERTS), gu.rearrange("e h n -> h e n")).then_inc(gu_in, 16)
            sp.dma_start(dn_sb[:].rearrange("p (e c h) -> p e c h", e=EXPERTS, c=2),
                         dn.rearrange("e (c p) h -> p e c h", p=P)).then_inc(dn_in, 16)
            for h in range(2):
                sp.wait_ge(out_ready, h + 1)
                sp.dma_start(out_v[:, h * HALF:(h + 1) * HALF], out_sb[:, h * HALF:(h + 1) * HALF]).then_inc(out_done, 16)
            sp.wait_ge(out_done, 32)

        @block.gpsimd
        def _(pool):
            nc.gpsimd.memset(ident[:], 0.0).then_inc(const_ready, 1)
            nc.gpsimd.memset(minus_half[:], -0.5).then_inc(const_ready, 1)
            pool.wait_ge(const_ready, 2)
            nc.gpsimd.affine_select(out=ident[:], in_=ident[:], compare_op=ALU.not_equal, fill=1.0, base=0,
                                    pattern=[[-1, P]], channel_multiplier=1).then_inc(const_ready, 1)

            def inverse_root(dst, src, n, ready, k, then):
                pool.wait_ge(ready, k)
                nc.gpsimd.tensor_tensor(dst, src, minus_half[:, 0:n], ALU.pow).then_inc(then, 1)

            inverse_root(rstd[:, 0:TPB], ve[:, 0:TPB], TPB, var_ready, 1, rstd_ready)
            inverse_root(rstd[:, TPB:TILES], ve[:, TPB:TILES], TILES - TPB, var_ready, 2, rstd_ready)
            nc.gpsimd.memset(e_base[:], E_BASE).then_inc(const_ready, 1)
            nc.gpsimd.memset(before[:], 1.0).then_inc(const_ready, 1)
            pool.wait_ge(const_ready, 5)
            nc.gpsimd.affine_select(out=before[:], in_=before[:], compare_op=ALU.is_gt, fill=0.0, base=0,
                                    pattern=[[1, EXPERTS], [-1, EXPERTS]], channel_multiplier=0).then_inc(const_ready, 1)
            pool.wait_ge(v_in, 32)
            nc.gpsimd.tensor_tensor(xb[:], x_sb[:], bv_sb[:].unsqueeze(1).to_broadcast([P, TILES, DIM]),
                                    ALU.add).then_inc(xb_ready, 1)

            def router_exp(h):
                s = slice(h * HALF, (h + 1) * HALF)
                pool.wait_ge(ldiff_ready, h + 1)
                nc.gpsimd.tensor_tensor(ex[:, s, :], e_base[:].rearrange("p (t e) -> p t e", e=EXPERTS),
                                        logit[:, s, :], ALU.pow).then_inc(exp_ready, 1)

            for b in range(BATCHES):
                s = slice(b * TPB, (b + 1) * TPB)
                inverse_root(rstd2[:, s], ve2[:, s], TPB, var2_ready, b + 1, rstd2_ready)
                if b == BATCHES // 2 - 1:
                    router_exp(0)
            router_exp(1)

            def add_expert(step, k):
                _, h = PAIR_STEPS[k]
                pool.wait_ge(y_scaled, step + 1)
                acc = x1[:, h * HALF:(h + 1) * HALF, :].rearrange("p t d -> p (t d)")
                if not isinstance(step, int) or step >= 1:
                    pool.wait_ge(y_added, step)
                nc.gpsimd.tensor_tensor(acc, acc, y_sb[:, k % 2, :], ALU.add).then_inc(y_added, 1)

            for k in range(4):
                add_expert(k, k)
            with pool.Fori(1, PAIRS) as i:
                for k in range(4):
                    add_expert(i * 4 + k, k)

        @block.scalar
        def _(act):
            act.dma_start(wq_sb[:], wq).then_inc(qk_in, 16)
            act.dma_start(wkT_sb[:], wkT).then_inc(qk_in, 16)
            act.dma_start(bqk_sb[:], bqk).then_inc(qk_in, 16)
            act.dma_start(wv_sb[:], wv).then_inc(v_in, 16)
            act.dma_start(bv_sb[:], bv.partition_broadcast(P)).then_inc(v_in, 16)
            act.dma_start(wr_sb[:], wrT).then_inc(route_in, 16)
            act.dma_start(rb_sb[:], rb.partition_broadcast(P)).then_inc(route_in, 16)
            act.dma_start(gub_sb[:], gub).then_inc(route_in, 16)
            act.dma_start(db_sb[:], db).then_inc(route_in, 16)

            def copy_xT(j):
                t0, n = PREP[j]
                act.wait_ge(xT_done, j + 1)
                nc.scalar.activation(xT[:, t0 * P:(t0 + n) * P], M[:, 0:n * P], ACT.Copy).then_inc(xT_copied, 1)

            def split_g(j):
                t0, n = PREP[j]
                act.wait_ge(g_done, j + 1)
                nc.scalar.activation(g_hi[:, t0 * P:(t0 + n) * P], M[:, 0:n * P], ACT.Copy).then_inc(g_hi_ready, 1)

            def split_ctx(b, g):
                t0, n = CTX_GROUPS[g]
                bank, before_it = T_USE["ctx", b, g]
                w = min(n * P, KEYS - t0 * P)
                act.wait_ge(t_done[bank], before_it + 1)
                nc.scalar.activation(ct_hi[b % 2][:, t0 * P:t0 * P + w], T[bank][:, 0:w], ACT.Copy).then_inc(ct_hi_ready, 1)

            def exponentials(b, q):
                n = b * TPB + q
                act.wait_ge(clipped, n + 1)
                act.wait_ge(negmax_ready, n + 1)
                nc.scalar.activation(pr[:, b % 2, q, 0:KEYS], sc[:, q, 0:KEYS], ACT.Exp, bias=neg_max[:, n:n + 1],
                                     accum_out=row_sum[:, n:n + 1]).then_inc(p_ready, 1)

            def copy_pT(b, g):
                t0, n = PT_GROUPS[g]
                bank, before_it = T_USE["pt", b, g]
                rows = P if t0 < KT_FULL else K_REST
                act.wait_ge(t_done[bank], before_it + 1)
                nc.scalar.activation(pT[0:rows, t0:t0 + n, :].rearrange("p t q -> p (t q)"), T[bank][0:rows, 0:n * TPB * P],
                                     ACT.Copy).then_inc(t_free[bank], 1)

            def copy_oT(b):
                act.wait_ge(o_done, b + 1)
                nc.scalar.activation(oT[:], O[:, 0:TPB * P], ACT.Copy).then_inc(oT_copied, 1)

            def split_x2(b):
                act.wait_ge(x2_done, b + 1)
                nc.scalar.activation(x2_hi[:, b * QUERIES:(b + 1) * QUERIES], M[:, 0:QUERIES], ACT.Copy).then_inc(x2_hi_ready, 1)

            copy_xT(0)
            for g in range(4):
                split_ctx(0, g)
            split_g(0)
            for b in range(BATCHES):
                if b + 1 < len(PREP):
                    copy_xT(b + 1)
                if b + 1 < BATCHES:
                    split_ctx(b + 1, 0)
                    split_ctx(b + 1, 1)
                exponentials(b, 0)
                if b + 1 < BATCHES:
                    split_ctx(b + 1, 2)
                    split_ctx(b + 1, 3)
                if b + 1 < len(PREP):
                    split_g(b + 1)
                exponentials(b, 1)
                if b >= 2:
                    split_x2(b - 2)
                if b >= 1:
                    for g in range(0, len(PT_GROUPS), 2):
                        copy_pT(b - 1, g)
                    copy_oT(b - 1)
            last = BATCHES - 1
            for g in range(0, len(PT_GROUPS), 2):
                copy_pT(last, g)
                if g == 4:
                    split_x2(last - 1)
            copy_oT(last)

            def expert(step, k, col):
                for ih in range(2):
                    act.wait_ge(gu_done, step * 4 + 2 * ih + 2)
                    if not isinstance(step, int) or step >= 2:
                        act.wait_ge(act_ready, step * 2 - 2)
                    nc.scalar.activation(up[:, k % 2, ih, :], S[2 * ih + 1][:], ACT.Identity,
                                         bias=gub1_sb[:, bass.ds(col + 2 + ih, 1)]).then_inc(up_copied, 1)
                    act.wait_ge(gate_copied, step * 2 + ih + 1)
                    nc.scalar.activation(gate[:, k % 2, ih, :], gate[:, k % 2, ih, :], ACT.Silu,
                                         scale=ALPHA).then_inc(silu_ready, 1)

            def scale_y(step, k, e):
                _, h = PAIR_STEPS[k]
                act.wait_ge(y_done, step + 1)
                if not isinstance(step, int) or step >= 2:
                    act.wait_ge(y_added, step - 1)
                for t in range(HALF):
                    n = h * HALF + t
                    ins = nc.scalar.activation(y_sb[:, k % 2, t * DIM:(t + 1) * DIM], T[k % 2][:, t * DIM:(t + 1) * DIM],
                                               ACT.Copy, scale=w_scaled[:, bass.ds(e * TILES + n, 1)])
                ins.then_inc(y_scaled, 1)

            act.wait_ge(gub1_ready, 1)
            expert(0, 0, 0)
            split_x2(last)
            expert(1, 1, 4)
            for k in range(4):
                e, h = PAIR_STEPS[k]
                act.wait_ge(route_ready, h + 1)
                scale_y(k, k, e)
                s = k + 2
                expert(s, s % 4, (s // 4 * 2 + PAIR_STEPS[s % 4][0]) * 4)
            with act.Fori(1, PAIRS - 1) as i:
                for k in range(4):
                    scale_y(i * 4 + k, k, i * 2 + PAIR_STEPS[k][0])
                    s = k + 2
                    expert(i * 4 + s, s % 4, i * 8 + (s // 4 * 2 + PAIR_STEPS[s % 4][0]) * 4)
            i = PAIRS - 1
            for k in range(4):
                scale_y(i * 4 + k, k, i * 2 + PAIR_STEPS[k][0])
                s = k + 2
                if s < 4:
                    expert(i * 4 + s, s, (i * 2 + PAIR_STEPS[s][0]) * 4)
                if k == 0:
                    for h, bank in enumerate((O, M)):
                        act.wait_ge(wT_done, h + 1)
                        nc.scalar.activation(wT[:, h * HTOK:(h + 1) * HTOK], bank[0:EXPERTS, :], ACT.Copy).then_inc(wT_copied, 1)

        @block.vector
        def _(dve):
            links = [0]

            def link(ins):
                links[0] += 1
                ins.then_inc(chain, 1)
                dve.wait_ge(chain, links[0])

            def moments(src, st, m, v, t0, n, then):
                for t in range(t0, t0 + n):
                    ins = nc.vector.bn_stats(st[:, t, :], src[:, t, :])
                link(ins)
                for t in range(t0, t0 + n):
                    ins = nc.vector.bn_aggr(m[:, t, :], st[:, t, :])
                link(ins)
                nc.vector.tensor_scalar(v[:, t0:t0 + n], m[:, t0:t0 + n, 1], EPS, None, ALU.add).then_inc(then, 1)

            def normalise(dst, src, m, r, t0, n, ready, k, then):
                dve.wait_ge(ready, k)
                for t in range(t0, t0 + n):
                    ins = nc.vector.tensor_scalar(dst[:, t, :], src[:, t, :], m[:, t, 0:1], r[:, t:t + 1],
                                                  ALU.subtract, ALU.mult)
                ins.then_inc(then, 1)

            def evict_q(j):
                t0, n = PREP[j]
                dve.wait_ge(q_done, j + 1)
                nc.vector.tensor_scalar(qT[:, t0 * P:(t0 + n) * P], M[:, 0:n * P], bqk_sb[:, 0:1], SCALE,
                                        ALU.add, ALU.mult).then_inc(q_copied, 1)

            def split_g(j):
                t0, n = PREP[j]
                s = slice(t0 * P, (t0 + n) * P)
                dve.wait_ge(g_hi_ready, j + 1)
                nc.vector.tensor_tensor(g_lo[:, s], M[:, 0:n * P], g_hi[:, s].bitcast(F32), ALU.subtract)
                nc.vector.tensor_scalar(clip_hi[:, t0:t0 + n], M[:, 3 * P:3 * P + n], -1.0, CLIP, ALU.mult, ALU.add)
                nc.vector.tensor_scalar(row_max[:, t0:t0 + n, NCH], M[:, 3 * P:3 * P + n], -1.0, -CLIP,
                                        ALU.mult, ALU.add).then_inc(g_lo_ready, 1)

            def split_ctx(b, g, k):
                t0, n = CTX_GROUPS[g]
                bank, _ = T_USE["ctx", b, g]
                w = min(n * P, KEYS - t0 * P)
                s = slice(t0 * P, t0 * P + w)
                dve.wait_ge(ct_hi_ready, b * len(CTX_GROUPS) + g + 1)
                nc.vector.tensor_tensor(ct_lo[b % 2][:, s], T[bank][:, 0:w], ct_hi[b % 2][:, s].bitcast(F32),
                                        ALU.subtract).then_inc(t_free[bank], 1)

            def clip_scores(b, q, chunks):
                n = b * TPB + q
                if chunks[0] == 0:
                    dve.wait_ge(g_lo_ready, prep_of(n) + 1)
                    if b >= 1:
                        dve.wait_ge(p_ready, n - TPB + 1)
                for c in chunks:
                    c0, w, _ = SCORE_CHUNKS[c]
                    dve.wait_ge(s_done, n * NCH + c + 1)
                    nc.vector.tensor_scalar(sc[:, q, c0:c0 + w], S[c][:, 0:w], clip_hi[:, n:n + 1], None, ALU.min, ALU.max,
                                            accum_out=row_max[:, n, c:c + 1]).then_inc(s_free, 1)
                if chunks[-1] == NCH - 1:
                    dve.wait_ge(s_free, (n + 1) * NCH)
                    nc.vector.tensor_reduce(neg_max[:, n:n + 1], row_max[:, n, :], AX.X, ALU.max, negate=True).then_inc(negmax_ready, 1)
                    nc.vector.tensor_scalar(sc[:, q, 0:KEYS], sc[:, q, 0:KEYS], row_max[:, n, NCH:NCH + 1], None,
                                            ALU.max).then_inc(clipped, 1)

            def copy_pT(b, g):
                t0, n = PT_GROUPS[g]
                bank, before_it = T_USE["pt", b, g]
                dve.wait_ge(t_done[bank], before_it + 1)
                nc.vector.tensor_copy(pT[:, t0:t0 + n, :].rearrange("p t q -> p (t q)"),
                                      T[bank][:, 0:n * TPB * P]).then_inc(t_free[bank], 1)

            def residual(b):
                s = slice(b * TPB, (b + 1) * TPB)
                dve.wait_ge(p_ready, (b + 1) * TPB)
                link(nc.vector.reciprocal(inv_sum[:, s], row_sum[:, s]))
                dve.wait_ge(v_done, b + 1)
                dve.wait_ge(xb_ready, 1)
                for q in range(TPB):
                    n = b * TPB + q
                    ins = nc.vector.scalar_tensor_tensor(x1[:, n, :], O[:, q * DIM:(q + 1) * DIM], inv_sum[:, n:n + 1],
                                                         xb[:, n, :], ALU.mult, ALU.add)
                ins.then_inc(x1_ready, 1)
                dve.wait_ge(x1_ready, b + 1)
                moments(x1, stats2, mv2, ve2, b * TPB, TPB, var2_ready)

            def split_x2(b):
                s = slice(b * QUERIES, (b + 1) * QUERIES)
                dve.wait_ge(x2_hi_ready, b + 1)
                nc.vector.tensor_tensor(x2_lo[:, s], M[:, 0:QUERIES], x2_hi[:, s].bitcast(F32),
                                        ALU.subtract).then_inc(x2_lo_ready, 1)

            def add_router_bias(b):
                s = slice(b * TPB, (b + 1) * TPB)
                dve.wait_ge(r_done, b + 1)
                dve.wait_ge(route_in, 64)
                nc.vector.tensor_tensor(logit[:, s, :], M[:, 0:TPB * EXPERTS].rearrange("p (t e) -> p t e", e=EXPERTS),
                                        rb_sb[:].unsqueeze(1).to_broadcast([P, TPB, EXPERTS]), ALU.add).then_inc(logit_ready, 1)

            def route(h):
                s = slice(h * HALF, (h + 1) * HALF)
                over = [P, HALF, EXPERTS]
                dve.wait_ge(logit_ready, (h + 1) * HALF // TPB)
                link(nc.vector.tensor_reduce(lmax[:, s], logit[:, s, :], AX.X, ALU.max))
                nc.vector.tensor_tensor(logit[:, s, :], logit[:, s, :], lmax[:, s].unsqueeze(2).to_broadcast(over),
                                        ALU.subtract).then_inc(ldiff_ready, 1)
                dve.wait_ge(exp_ready, h + 1)
                link(nc.vector.tensor_reduce(esum[:, s], ex[:, s, :], AX.X, ALU.add))
                link(nc.vector.reciprocal(esum[:, s], esum[:, s]))
                link(nc.vector.tensor_tensor(prob[:, s, :], ex[:, s, :], esum[:, s].unsqueeze(2).to_broadcast(over), ALU.mult))
                cube = [P, HALF, EXPERTS, EXPERTS]
                b4 = beats[:].rearrange("p (t e) j -> p t e j", e=EXPERTS)
                t4 = ties[:].rearrange("p (t e) j -> p t e j", e=EXPERTS)
                other, own = prob[:, s, :].unsqueeze(2).to_broadcast(cube), prob[:, s, :].unsqueeze(3).to_broadcast(cube)
                dve.wait_ge(const_ready, SETUP_CONSTS)
                link(nc.vector.tensor_tensor(t4, other, own, ALU.is_equal))
                nc.vector.tensor_tensor(b4, other, own, ALU.is_gt)
                link(nc.vector.tensor_tensor(t4, t4, before[:].unsqueeze(1).to_broadcast(cube), ALU.mult))
                link(nc.vector.tensor_tensor(beats[:], beats[:], ties[:], ALU.add))
                link(nc.vector.tensor_reduce(rank[:, s, :], b4, AX.X, ALU.add))
                link(nc.vector.scalar_tensor_tensor(w_route[:, s, :], rank[:, s, :], float(TOP_K), prob[:, s, :],
                                                    ALU.is_lt, ALU.mult))
                nc.vector.tensor_scalar(w_scaled[:].rearrange("p (e t) -> p t e", t=TILES)[:, s, :], w_route[:, s, :],
                                        1.0 / ALPHA, None, ALU.mult).then_inc(route_ready, 1)

            def split_w(e, buf, ready):
                src = gu_sb[:, bass.ds(e * (2 * HIDDEN), 2 * HIDDEN)]
                nc.vector.tensor_copy(w_hi[buf][:], src).then_inc(w_hi_ready, 1)
                dve.wait_ge(w_hi_ready, e + 1)
                nc.vector.tensor_tensor(w_lo[buf][:], src, w_hi[buf][:].bitcast(F32), ALU.subtract).then_inc(w_ready, 1)

            def prep_of(n):
                return next(j for j, (t0, m) in enumerate(PREP) if t0 <= n < t0 + m)

            for i in range(2):
                nc.vector.memset(ct_hi[i][:, KEYS:KEYS_EVEN].bitcast(F32), 0.0)
                ins = nc.vector.memset(ct_lo[i][:, KEYS:KEYS_EVEN].bitcast(F32), 0.0)
            ins.then_inc(pad_ready, 1)
            dve.wait_ge(x0_in, 16)
            moments(x_sb, stats, mv, ve, 0, TPB, var_ready)
            normalise(xn, x_sb, mv, rstd, 0, TPB, rstd_ready, 1, xn_ready)
            dve.wait_ge(x1_in, 16)
            moments(x_sb, stats, mv, ve, TPB, TILES - TPB, var_ready)
            split_ctx(0, 0, 0)
            split_ctx(0, 1, 0)
            dve.wait_ge(qk_in, 48)
            evict_q(0)
            split_ctx(0, 2, 0)
            split_ctx(0, 3, 0)
            split_g(0)
            normalise(xn, x_sb, mv, rstd, TPB, TILES - TPB, rstd_ready, 2, xn_ready)
            dve.wait_ge(route_in, 64)
            nc.vector.tensor_scalar(gub1_sb[:], gub_sb[:], 1.0, None, ALU.add).then_inc(gub1_ready, 1)
            link(nc.vector.tensor_copy(wr_hi[:], wr_sb[:]))
            nc.vector.tensor_tensor(wr_lo[:], wr_sb[:], wr_hi[:].bitcast(F32), ALU.subtract)
            for b in range(BATCHES):
                clip_scores(b, 0, range(NCH))
                if b >= 2:
                    residual(b - 2)
                if b + 1 < BATCHES:
                    split_ctx(b + 1, 0, 0)
                    split_ctx(b + 1, 1, 0)
                clip_scores(b, 1, range(0, 2))
                if b + 1 < len(PREP):
                    evict_q(b + 1)
                clip_scores(b, 1, range(2, NCH))
                if b >= 2:
                    normalise(xn2, x1, mv2, rstd2, (b - 2) * TPB, TPB, rstd2_ready, b - 1, xn2_ready)
                if b + 1 < BATCHES:
                    split_ctx(b + 1, 2, 0)
                    split_ctx(b + 1, 3, 0)
                if b + 1 < len(PREP):
                    split_g(b + 1)
                if b >= 2:
                    split_x2(b - 2)
                if b >= 1:
                    copy_pT(b - 1, 1)
                    if b >= 2:
                        add_router_bias(b - 2)
                    copy_pT(b - 1, 3)
                    copy_pT(b - 1, 5)
                if b == 1:
                    dve.wait_ge(gu_in, 16)
                    split_w(0, 0, w_ready)
                    split_w(1, 1, w_ready)
                if b == 3:
                    route(0)
            last = BATCHES - 1
            residual(last - 1)
            copy_pT(last, 1)
            normalise(xn2, x1, mv2, rstd2, (last - 1) * TPB, TPB, rstd2_ready, last, xn2_ready)
            copy_pT(last, 3)
            split_x2(last - 1)
            copy_pT(last, 5)
            add_router_bias(last - 1)
            residual(last)

            def expert(step, k, col, split=None):
                for ih in range(2):
                    dve.wait_ge(gu_done, step * 4 + 2 * ih + 1)
                    nc.vector.tensor_scalar(gate[:, k % 2, ih, :], S[2 * ih][:], gub_sb[:, bass.ds(col + ih, 1)], LIMIT,
                                            ALU.add, ALU.min).then_inc(gate_copied, 1)
                    dve.wait_ge(up_copied, step * 2 + ih + 1)
                    nc.vector.tensor_scalar(up[:, k % 2, ih, :], up[:, k % 2, ih, :], 1.0 + LIMIT, 1.0 - LIMIT,
                                            ALU.min, ALU.max).then_inc(up_clipped, 1)
                if split is not None:
                    dve.wait_ge(gu_done, step * 4 + 4)
                    split_w(split, k % 2, w_ready)
                for ih in range(2):
                    dve.wait_ge(up_clipped, step * 2 + ih + 1)
                    dve.wait_ge(silu_ready, step * 2 + ih + 1)
                    if not isinstance(step, int) or step >= 2:
                        dve.wait_ge(y_done, step - 1)
                    nc.vector.tensor_tensor(act_t[k % 2][:, ih, :], up[:, k % 2, ih, :], gate[:, k % 2, ih, :],
                                            ALU.mult).then_inc(act_ready, 1)

            expert(0, 0, 0)
            normalise(xn2, x1, mv2, rstd2, last * TPB, TPB, rstd2_ready, BATCHES, xn2_ready)
            split_x2(last)
            expert(1, 1, 4)
            add_router_bias(last)
            route(1)
            expert(2, 2, 0, split=2)
            expert(3, 3, 4, split=3)
            with dve.Fori(1, PAIRS - 1) as i:
                for k in range(4):
                    e, h = PAIR_STEPS[k]
                    expert(i * 4 + k, k, i * 8 + e * 4, split=i * 2 + 2 + e if h == 1 else None)
            i = PAIRS - 1
            for k in range(4):
                expert(i * 4 + k, k, i * 8 + PAIR_STEPS[k][0] * 4)
            for h, bank in enumerate((O, M)):
                dve.wait_ge(db_done, h + 1)
                dve.wait_ge(y_added, STEPS - 2 + 2 * h)
                s = slice(h * HALF, (h + 1) * HALF)
                nc.vector.tensor_tensor(out_sb[:, s, :], bank[:].rearrange("p (t d) -> p t d", d=DIM), x1[:, s, :],
                                        ALU.add).then_inc(out_ready, 1)

        @block.tensor
        def _(pe):
            def three(dst, a_hi, a_lo, b_hi, b_lo):
                nc.tensor.matmul(dst, a_hi, b_hi, start=True, stop=False)
                nc.tensor.matmul(dst, a_hi, b_lo, start=False, stop=False)
                return nc.tensor.matmul(dst, a_lo, b_hi, start=False, stop=True)

            def transpose_xn(j):
                t0, n = PREP[j]
                if j == 0:
                    pe.wait_ge(const_ready, 3)
                else:
                    pe.wait_ge(g_lo_ready, j)
                pe.wait_ge(xn_ready, min(j, 1) + 1)
                for t in range(n):
                    ins = nc.tensor.transpose(M[:, t * P:(t + 1) * P], xn[:, t0 + t, :], ident[:])
                ins.then_inc(xT_done, 1)

            def project_q(j):
                t0, n = PREP[j]
                pe.wait_ge(qk_in, 48)
                pe.wait_ge(xT_copied, j + 1)
                nc.tensor.matmul(M[:, 0:n * P], wq_sb[:], xT[:, t0 * P:(t0 + n) * P], start=True, stop=True).then_inc(q_done, 1)

            def fold_keys(j):
                t0, n = PREP[j]
                pe.wait_ge(q_copied, j + 1)
                nc.tensor.matmul(M[:, 0:n * P], wkT_sb[:], qT[:, t0 * P:(t0 + n) * P], start=True, stop=True)
                for t in range(n):
                    ins = nc.tensor.matmul(M[:, 3 * P + t:3 * P + t + 1], qT[:, (t0 + t) * P:(t0 + t + 1) * P],
                                           bqk_sb[:, 1:2], start=True, stop=True)
                ins.then_inc(g_done, 1)

            def transpose_ctx(b, g):
                t0, n = CTX_GROUPS[g]
                bank, before_it = T_USE["ctx", b, g]
                pe.wait_ge(ctx_in_s[b], 32)
                if before_it:
                    pe.wait_ge(t_free[bank], before_it)
                for t in range(t0, t0 + n):
                    rows = P if t < KT_FULL else K_REST
                    ins = nc.tensor.transpose(T[bank][:, (t - t0) * P:(t - t0) * P + rows], ctx_sb[b][0:rows, t, :],
                                              ident[0:rows, 0:rows])
                ins.then_inc(t_done[bank], 1)

            def scores(b, q, chunks):
                n = b * TPB + q
                tok = slice(n * P, (n + 1) * P)
                if q == 0 and chunks[0] == 0:
                    for bank in range(2):
                        g = len(CTX_GROUPS) - 2 + bank
                        pe.wait_ge(t_free[bank], T_USE["ctx", b, g][1] + 1)
                    pe.wait_ge(pad_ready, 1)
                if chunks[0] == 0:
                    pe.wait_ge(g_lo_ready, next(j for j, (t0, m) in enumerate(PREP) if t0 <= n < t0 + m) + 1)
                for c in chunks:
                    c0, _, w = SCORE_CHUNKS[c]
                    if n:
                        pe.wait_ge(s_free, (n - 1) * NCH + c + 1)
                    three(S[c][:, 0:w], g_hi[:, tok], g_lo[:, tok], ct_hi[b % 2][:, c0:c0 + w],
                          ct_lo[b % 2][:, c0:c0 + w]).then_inc(s_done, 1)

            def transpose_p(b, g):
                t0, n = PT_GROUPS[g]
                bank, before_it = T_USE["pt", b, g]
                pe.wait_ge(p_ready, (b + 1) * TPB)
                pe.wait_ge(t_free[bank], before_it)
                for t in range(t0, t0 + n):
                    rows = P if t < KT_FULL else K_REST
                    for q in range(TPB):
                        at = ((t - t0) * TPB + q) * P
                        ins = nc.tensor.transpose(T[bank][0:rows, at:at + P], pr[:, b % 2, q, t * P:t * P + rows], ident[:])
                ins.then_inc(t_done[bank], 1)

            def weighted_sum(b, g):
                t0, n = PT_GROUPS[g]
                bank, before_it = T_USE["pt", b, g]
                pe.wait_ge(t_free[bank], before_it + 1)
                if g == 0 and b:
                    pe.wait_ge(x1_ready, b)
                for t in range(t0, t0 + n):
                    rows = P if t < KT_FULL else K_REST
                    ins = nc.tensor.matmul(O[:, 0:TPB * P], ctx_sb[b][0:rows, t, :], pT[0:rows, t, :],
                                           start=(t == 0), stop=(t == KT - 1))
                if t == KT - 1:
                    ins.then_inc(o_done, 1)

            def project_v(b):
                pe.wait_ge(v_in, 32)
                pe.wait_ge(oT_copied, b + 1)
                for q in range(TPB):
                    ins = nc.tensor.matmul(O[:, q * DIM:(q + 1) * DIM], oT[:, q * P:(q + 1) * P], wv_sb[:], start=True, stop=True)
                ins.then_inc(v_done, 1)

            def transpose_x2(b):
                pe.wait_ge(xn2_ready, b + 1)
                if b:
                    pe.wait_ge(logit_ready, b)
                for q in range(TPB):
                    ins = nc.tensor.transpose(M[:, q * P:(q + 1) * P], xn2[:, b * TPB + q, :], ident[:])
                ins.then_inc(x2_done, 1)

            def router(b):
                pe.wait_ge(x2_lo_ready, b + 1)
                for q in range(TPB):
                    tok = slice((b * TPB + q) * P, (b * TPB + q + 1) * P)
                    ins = three(M[:, q * EXPERTS:(q + 1) * EXPERTS], x2_hi[:, tok], x2_lo[:, tok], wr_hi[:], wr_lo[:])
                ins.then_inc(r_done, 1)

            transpose_xn(0)
            transpose_ctx(0, 0)
            transpose_ctx(0, 1)
            project_q(0)
            transpose_ctx(0, 2)
            transpose_ctx(0, 3)
            fold_keys(0)
            for b in range(BATCHES):
                scores(b, 0, range(0, 2))
                if b >= 2:
                    project_v(b - 2)
                scores(b, 0, range(2, NCH))
                if b + 1 < len(PREP):
                    transpose_xn(b + 1)
                if b + 1 < BATCHES:
                    transpose_ctx(b + 1, 0)
                    transpose_ctx(b + 1, 1)
                scores(b, 1, range(0, 2))
                if b + 1 < len(PREP):
                    project_q(b + 1)
                scores(b, 1, range(2, NCH))
                if b + 1 < BATCHES:
                    transpose_ctx(b + 1, 2)
                    transpose_ctx(b + 1, 3)
                if b + 1 < len(PREP):
                    fold_keys(b + 1)
                if b >= 2:
                    transpose_x2(b - 2)
                if b >= 1:
                    transpose_p(b - 1, 0)
                    transpose_p(b - 1, 1)
                    if b >= 2:
                        router(b - 2)
                    for g in range(len(PT_GROUPS)):
                        weighted_sum(b - 1, g)
                        if g + 2 < len(PT_GROUPS):
                            transpose_p(b - 1, g + 2)
            last = BATCHES - 1
            project_v(last - 1)
            transpose_p(last, 0)
            transpose_p(last, 1)
            for g in range(len(PT_GROUPS)):
                weighted_sum(last, g)
                if g + 2 < len(PT_GROUPS):
                    transpose_p(last, g + 2)
                if g == 3:
                    transpose_x2(last - 1)
            router(last - 1)

            def gate_up(step, k, ih, loads):
                _, h = PAIR_STEPS[k]
                tok = slice(h * HTOK, (h + 1) * HTOK)
                buf = k % 2
                if ih == 0:
                    pe.wait_ge(w_ready, loads)
                for part in range(2):
                    if isinstance(step, int) and step == 0:
                        if ih == 0 and part == 0:
                            pe.wait_ge(s_free, TILES * NCH)
                    else:
                        pe.wait_ge(up_copied if part else gate_copied, step * 2 + ih - 1)
                    col = slice((part * 2 + ih) * P, (part * 2 + ih + 1) * P)
                    three(S[2 * ih + part][:], w_hi[buf][:, col], w_lo[buf][:, col], x2_hi[:, tok], x2_lo[:, tok]).then_inc(gu_done, 1)

            def down(step, k, e):
                if isinstance(step, int) and step < 2:
                    pe.wait_ge(t_free[k % 2], T_TOTAL[k % 2])
                else:
                    pe.wait_ge(y_scaled, step - 1)
                for t in range(HALF):
                    for ih in range(2):
                        if t == 0:
                            pe.wait_ge(act_ready, step * 2 + ih + 1)
                        ins = nc.tensor.matmul(T[k % 2][:, t * DIM:(t + 1) * DIM], act_t[k % 2][:, ih, t * P:(t + 1) * P],
                                               dn_sb[:, bass.ds((e * 2 + ih) * DIM, DIM)], start=(ih == 0), stop=(ih == 1))
                ins.then_inc(y_done, 1)

            gate_up(0, 0, 0, 1)
            project_v(last)
            gate_up(0, 0, 1, 1)
            gate_up(1, 1, 0, 2)
            gate_up(1, 1, 1, 2)
            transpose_x2(last)
            router(last)
            pe.wait_ge(dn_in, 16)
            for k in range(4):
                down(k, k, PAIR_STEPS[k][0])
                s = k + 2
                for ih in range(2):
                    gate_up(s, s % 4, ih, s // 4 * 2 + PAIR_STEPS[s % 4][0] + 1)
            with pe.Fori(1, PAIRS - 1) as i:
                for k in range(4):
                    down(i * 4 + k, k, i * 2 + PAIR_STEPS[k][0])
                    s = k + 2
                    for ih in range(2):
                        gate_up(i * 4 + s, s % 4, ih, i * 2 + s // 4 * 2 + PAIR_STEPS[s % 4][0] + 1)
            i = PAIRS - 1
            for k in range(4):
                down(i * 4 + k, k, i * 2 + PAIR_STEPS[k][0])
                s = k + 2
                if s < 4:
                    for ih in range(2):
                        gate_up(i * 4 + s, s, ih, i * 2 + PAIR_STEPS[s][0] + 1)
                if k == 0:
                    pe.wait_ge(logit_ready, BATCHES)
                    pe.wait_ge(route_ready, 2)
                    for h, bank in enumerate((O, M)):
                        for t in range(HALF):
                            ins = nc.tensor.transpose(bank[0:EXPERTS, t * P:(t + 1) * P], w_route[:, h * HALF + t, :], ident[:])
                        ins.then_inc(wT_done, 1)
                if k == 1:
                    pe.wait_ge(route_in, 64)
                    for h, bank in enumerate((O, M)):
                        pe.wait_ge(wT_copied, h + 1)
                        for t in range(HALF):
                            n = h * HALF + t
                            ins = nc.tensor.matmul(bank[:, t * DIM:(t + 1) * DIM], wT[:, n * P:(n + 1) * P], db_sb[:],
                                                   start=True, stop=True)
                        ins.then_inc(db_done, 1)


def kernel(x, ctx_1024, L0_xattn_Wq, L0_xattn_bq, L0_xattn_Wk, L0_xattn_bk, L0_xattn_Wv, L0_xattn_bv,
           L0_ffn_router_weight, L0_ffn_router_bias, L0_ffn_gate_up_proj, L0_ffn_gate_up_bias,
           L0_ffn_down_proj, L0_ffn_down_bias):
    import concourse.bacc as bacc
    from concourse.bass_utils import run_bass_kernel_spmd

    a = np.ascontiguousarray
    arrays = {
        "in_x": a(x), "in_ctx": a(ctx_1024), "in_wq": a(L0_xattn_Wq), "in_wkT": a(np.asarray(L0_xattn_Wk).T),
        "in_bqk": a(np.stack([np.asarray(L0_xattn_bq), np.asarray(L0_xattn_bk)], axis=1)),
        "in_wv": a(L0_xattn_Wv), "in_bv": a(L0_xattn_bv),
        "in_wrT": a(np.asarray(L0_ffn_router_weight).T), "in_rb": a(L0_ffn_router_bias),
        "in_gu": a(L0_ffn_gate_up_proj),
        "in_gub": a(np.asarray(L0_ffn_gate_up_bias).reshape(EXPERTS * 4, P).T),
        "in_dn": a(L0_ffn_down_proj), "in_db": a(L0_ffn_down_bias),
    }
    nc = bacc.Bacc("TRN2", target_bir_lowering=False, num_devices=1)
    args = [nc.dram_tensor(n, v.shape, mybir.dt.from_np(v.dtype), kind="ExternalInput").ap() for n, v in arrays.items()]
    out = nc.dram_tensor("out_x", (BATCHES, QUERIES, DIM), F32, kind="ExternalOutput").ap()
    build(nc, *args, out)
    r = run_bass_kernel_spmd(nc, [arrays], core_ids=[0])
    return r.results[0]["out_x"]
```

```python
import numpy as np
import concourse.bass as bass
from concourse import mybir
from contextlib import ExitStack

F32 = mybir.dt.float32
F32R = mybir.dt.float32r
ALU = mybir.AluOpType
ACT = mybir.ActivationFunctionType
AX = mybir.AxisListType

BATCHES, QUERIES, DIM = 4, 256, 128
KEYS = 1601
EXPERTS, HIDDEN, TOP_K = 8, 256, 2
P = 128
TILES = BATCHES * QUERIES // P
TPB = QUERIES // P
KT_FULL = KEYS // P
KT = KT_FULL + 1
K_REST = KEYS - KT_FULL * P
KEYS_EVEN = KEYS + KEYS % 2
SCALE = float(1.0 / np.sqrt(DIM).astype(np.float32))
CLIP = 100.0
EPS = 1e-5
ALPHA, LIMIT = 1.702, 7.0
E_BASE = float(np.float32(np.e))

_CW = KEYS // 4 // 2 * 2
SCORE_CHUNKS = [(c * _CW, _CW, _CW) for c in range(3)] + [(3 * _CW, KEYS - 3 * _CW, KEYS_EVEN - 3 * _CW)]
NCH = len(SCORE_CHUNKS)
PREP = [(0, 2), (2, 3), (5, 3)]
CTX_GROUPS = [(t, min(4, KT - t)) for t in range(0, KT, 4)]
PT_GROUPS = [(t, min(2, KT - t)) for t in range(0, KT, 2)]
PAIRS = EXPERTS // 2
WARM_UP = 10
HALF = TILES // 2
HTOK = HALF * P
STEPS = 2 * EXPERTS
PAIR_STEPS = [(0, 0), (1, 0), (0, 1), (1, 1)]


def _transpose_bank_uses():
    order = [("ctx", 0, g) for g in range(len(CTX_GROUPS))]
    for b in range(BATCHES + 1):
        for ctx_part, pt_part in (((0, 1), (0, 1, 2, 3)), ((2, 3), (4, 5, 6))):
            order += [("ctx", b + 1, g) for g in ctx_part if b + 1 < BATCHES]
            order += [("pt", b - 1, g) for g in pt_part if b >= 1]
    seen, found = [0, 0], {}
    for kind, b, g in order:
        found[kind, b, g] = (g % 2, seen[g % 2])
        seen[g % 2] += 1
    return found, seen


T_USE, T_TOTAL = _transpose_bank_uses()


def build(nc, x, ctx_in, att_w, more_w, rows, gu, dn, db, out):
    es = ExitStack()
    with es:
        def sb(name, shape, dt=F32):
            return es.enter_context(nc.sbuf_tensor(name, shape, dt))

        def sem(name):
            return es.enter_context(nc.semaphore(name))

        x_sb = sb("x_sb", [P, TILES, DIM])
        ctx_sb = [sb(f"ctx_sb{b}", [P, KT, DIM]) for b in range(BATCHES)]
        att_sb = sb("att_sb", [P, 2 * DIM + 2])
        wq_sb, wkT_sb, bqk_sb = att_sb[:, 0:DIM], att_sb[:, DIM:2 * DIM], att_sb[:, 2 * DIM:2 * DIM + 2]
        more_sb = sb("more_sb", [P, DIM + EXPERTS + EXPERTS * 4])
        wv_sb, wr_sb, gub_sb = more_sb[:, 0:DIM], more_sb[:, DIM:DIM + EXPERTS], more_sb[:, DIM + EXPERTS:]
        rows_sb = sb("rows_sb", [P, DIM + EXPERTS])
        bv_sb, rb_sb = rows_sb[:, 0:DIM], rows_sb[:, DIM:DIM + EXPERTS]
        bqs_sb = sb("bqs_sb", [P, 1])
        gu_sb = sb("gu_sb", [P, EXPERTS * 2 * HIDDEN])
        gub1_sb = sb("gub1_sb", [P, EXPERTS * 4])
        dn_sb = sb("dn_sb", [P, EXPERTS * 2 * DIM])
        db_sb = sb("db_sb", [EXPERTS, DIM])
        ident = sb("ident", [P, P])
        before = sb("before", [P, EXPERTS, EXPERTS])
        minus_half = sb("minus_half", [P, TILES])
        e_base = sb("e_base", [P, TPB * EXPERTS])
        stats = sb("stats", [P, TILES, 6])
        mv = sb("mv", [P, TILES, 2])
        ve = sb("ve", [P, TILES])
        rstd = sb("rstd", [P, TILES])
        xn = sb("xn", [P, TILES, DIM])
        stats2 = sb("stats2", [P, TILES, 6])
        mv2 = sb("mv2", [P, TILES, 2])
        ve2 = sb("ve2", [P, TILES])
        rstd2 = sb("rstd2", [P, TILES])
        xn2 = sb("xn2", [P, TILES, DIM])
        xT = sb("xT", [P, TILES * P])
        qT = sb("qT", [P, TILES * P])
        g_hi = sb("g_hi", [P, TILES * P], F32R)
        g_lo = sb("g_lo", [P, TILES * P], F32R)
        clip_hi = sb("clip_hi", [P, TILES])
        row_max = sb("row_max", [P, TILES, NCH + 1])
        neg_max = sb("neg_max", [P, TILES])
        row_sum = sb("row_sum", [P, TILES])
        inv_sum = sb("inv_sum", [P, TILES])
        ct_hi = [sb(f"ct_hi{i}", [P, KEYS_EVEN], F32R) for i in range(2)]
        ct_lo = [sb(f"ct_lo{i}", [P, KEYS_EVEN], F32R) for i in range(2)]
        sc = sb("sc", [P, TPB, KEYS_EVEN])
        pr = sb("pr", [P, 2, TPB, KEYS_EVEN])
        pT = sb("pT", [P, KT, TPB * P])
        oT = sb("oT", [P, TPB * P])
        xb = sb("xb", [P, TILES, DIM])
        x1 = sb("x1", [P, TILES, DIM])
        x2_hi = sb("x2_hi", [P, TILES * P], F32R)
        x2_lo = sb("x2_lo", [P, TILES * P], F32R)
        wr_hi = sb("wr_hi", [P, EXPERTS], F32R)
        wr_lo = sb("wr_lo", [P, EXPERTS], F32R)
        logit = sb("logit", [P, TILES, EXPERTS])
        lmax = sb("lmax", [P, TILES])
        ex = sb("ex", [P, TILES, EXPERTS])
        esum = sb("esum", [P, TILES])
        prob = sb("prob", [P, TILES, EXPERTS])
        beats = sb("beats", [P, HALF * EXPERTS, EXPERTS])
        ties = sb("ties", [P, HALF * EXPERTS, EXPERTS])
        rank = sb("rank", [P, TILES, EXPERTS])
        w_route = sb("w_route", [P, TILES, EXPERTS])
        w_scaled = sb("w_scaled", [P, TILES * EXPERTS])
        wT = sb("wT", [EXPERTS, TILES * P])
        w_hi = [sb(f"w_hi{i}", [P, 2 * HIDDEN], F32R) for i in range(2)]
        w_lo = [sb(f"w_lo{i}", [P, 2 * HIDDEN], F32R) for i in range(2)]
        gate = sb("gate", [P, 2, 2, HTOK])
        up = sb("up", [P, 2, 2, HTOK])
        act_t = [old[:].rearrange("p (c t) -> p c t", c=2) for old in (xT, qT)]
        y_sb = xn2[:].rearrange("p (k t) d -> p k (t d)", k=2)
        out_sb = xn

        S = [es.enter_context(nc.psum_tensor(f"S{i}", [P, 512], F32)) for i in range(4)]
        T = [es.enter_context(nc.psum_tensor(f"T{i}", [P, 512], F32)) for i in range(2)]
        O = es.enter_context(nc.psum_tensor("O", [P, 512], F32))
        M = es.enter_context(nc.psum_tensor("M", [P, 512], F32))

        bq_scaled = sem("bq_scaled")
        x0_in, x1_in, att_in, more_in = sem("x0_in"), sem("x1_in"), sem("att_in"), sem("more_in")
        ctx_in_s = [sem(f"ctx_in{b}") for b in range(BATCHES)]
        rows_in, db_in, gu_in, dn_in, out_done = sem("rows_in"), sem("db_in"), sem("gu_in"), sem("dn_in"), sem("out_done")
        const_ready = sem("const_ready")
        pad_ready = sem("pad_ready")
        var_ready, rstd_ready, xn_ready = sem("var_ready"), sem("rstd_ready"), sem("xn_ready")
        var2_ready, rstd2_ready, xn2_ready = sem("var2_ready"), sem("rstd2_ready"), sem("xn2_ready")
        xT_done, xT_copied, q_done, q_copied = sem("xT_done"), sem("xT_copied"), sem("q_done"), sem("q_copied")
        g_done, g_hi_ready, g_lo_ready, clip_ready = sem("g_done"), sem("g_hi_ready"), sem("g_lo_ready"), sem("clip_ready")
        t_done, t_free = [sem("t_done0"), sem("t_done1")], [sem("t_free0"), sem("t_free1")]
        ct_hi_ready = sem("ct_hi_ready")
        s_done, s_free = sem("s_done"), sem("s_free")
        negmax_ready, clipped, p_ready = sem("negmax_ready"), sem("clipped"), sem("p_ready")
        o_done, oT_copied, v_done, x1_ready = sem("o_done"), sem("oT_copied"), sem("v_done"), sem("x1_ready")
        xb_ready, inv_ready = sem("xb_ready"), sem("inv_ready")
        x2_done, x2_hi_ready, x2_lo_ready = sem("x2_done"), sem("x2_hi_ready"), sem("x2_lo_ready")
        r_done, logit_ready, ldiff_ready, exp_ready = sem("r_done"), sem("logit_ready"), sem("ldiff_ready"), sem("exp_ready")
        prob_ready, beats_ready, route_ready = sem("prob_ready"), sem("beats_ready"), sem("route_ready")
        chain = sem("chain")
        w_ready = sem("w_ready")
        w_hi_ready = sem("w_hi_ready")
        gub1_ready = sem("gub1_ready")
        gu_done, gate_copied, up_copied = sem("gu_done"), sem("gate_copied"), sem("up_copied")
        silu_ready, up_clipped, act_ready = sem("silu_ready"), sem("up_clipped"), sem("act_ready")
        y_done, y_scaled, y_added = sem("y_done"), sem("y_scaled"), sem("y_added")
        bias_added, y_tile_done = sem("bias_added"), sem("y_tile_done")
        wT_done, wT_copied, db_done, out_ready = sem("wT_done"), sem("wT_copied"), sem("db_done"), sem("out_ready")

        block = es.enter_context(nc.Block())

        x_v = x.rearrange("b (t p) d -> p (b t) d", p=P)
        out_v = out.rearrange("b (t p) d -> p (b t) d", p=P)
        SETUP_CONSTS = 6

        @block.sync
        def _(sp):
            sp.dma_start(x_sb[:, 0:TPB], x_v[:, 0:TPB]).then_inc(x0_in, 16)
            for b in range(BATCHES):
                sp.dma_start(ctx_sb[b][:, 0:KT_FULL, :],
                             ctx_in[b, 0:KT_FULL * P, :].rearrange("(p t) d -> p t d", t=KT_FULL)).then_inc(ctx_in_s[b], 16)
                sp.dma_start(ctx_sb[b][0:K_REST, KT_FULL, :], ctx_in[b, KT_FULL * P:KEYS, :]).then_inc(ctx_in_s[b], 16)
                if b == 0:
                    sp.dma_start(x_sb[:, TPB:TILES], x_v[:, TPB:TILES]).then_inc(x1_in, 16)
                    sp.dma_start(rows_sb[:], rows.partition_broadcast(P)).then_inc(rows_in, 16)
                    sp.dma_start(more_sb[:], more_w).then_inc(more_in, 16)
            sp.dma_start(gu_sb[:].rearrange("p (e n) -> p e n", e=EXPERTS), gu.rearrange("e h n -> h e n")).then_inc(gu_in, 16)
            sp.dma_start(dn_sb[:].rearrange("p (e c h) -> p e c h", e=EXPERTS, c=2),
                         dn.rearrange("e (c p) h -> p e c h", p=P)).then_inc(dn_in, 16)
            sp.dma_start(db_sb[:], db).then_inc(db_in, 16)
            sp.wait_ge(out_ready, 1)
            sp.dma_start(out_v[:, 0:HALF], out_sb[:, 0:HALF]).then_inc(out_done, 16)
            for t in range(HALF, TILES, 2):
                sp.wait_ge(out_ready, t - HALF + 3)
                sp.dma_start(out_v[:, t:t + 2], out_sb[:, t:t + 2]).then_inc(out_done, 16)
            sp.wait_ge(out_done, 48)

        @block.gpsimd
        def _(pool):
            nc.gpsimd.memset(ident[:], 0.0).then_inc(const_ready, 1)
            nc.gpsimd.memset(minus_half[:], -0.5).then_inc(const_ready, 1)
            pool.wait_ge(const_ready, 2)
            nc.gpsimd.affine_select(out=ident[:], in_=ident[:], compare_op=ALU.not_equal, fill=1.0, base=0,
                                    pattern=[[-1, P]], channel_multiplier=1).then_inc(const_ready, 1)

            def inverse_root(dst, src, n, ready, k, then):
                pool.wait_ge(ready, k)
                nc.gpsimd.tensor_tensor(dst, src, minus_half[:, 0:n], ALU.pow).then_inc(then, 1)

            inverse_root(rstd[:, 0:TPB], ve[:, 0:TPB], TPB, var_ready, 1, rstd_ready)
            for j in range(1, len(PREP)):
                t0, n = PREP[j]
                inverse_root(rstd[:, t0:t0 + n], ve[:, t0:t0 + n], n, var_ready, j + 1, rstd_ready)
            nc.gpsimd.memset(e_base[:], E_BASE).then_inc(const_ready, 1)
            nc.gpsimd.memset(before[:], 1.0).then_inc(const_ready, 1)
            pool.wait_ge(const_ready, 5)
            nc.gpsimd.affine_select(out=before[:], in_=before[:], compare_op=ALU.is_gt, fill=0.0, base=0,
                                    pattern=[[1, EXPERTS], [-1, EXPERTS]], channel_multiplier=0).then_inc(const_ready, 1)
            pool.wait_ge(rows_in, 16)
            nc.gpsimd.tensor_tensor(xb[:], x_sb[:], bv_sb.unsqueeze(1).to_broadcast([P, TILES, DIM]),
                                    ALU.add).then_inc(xb_ready, 1)

            def router_exponentials(b):
                s = slice(b * TPB, (b + 1) * TPB)
                pool.wait_ge(ldiff_ready, b + 1)
                nc.gpsimd.tensor_tensor(ex[:, s, :], e_base[:].rearrange("p (t e) -> p t e", e=EXPERTS),
                                        logit[:, s, :], ALU.pow).then_inc(exp_ready, 1)

            for b in range(BATCHES):
                s = slice(b * TPB, (b + 1) * TPB)
                inverse_root(rstd2[:, s], ve2[:, s], TPB, var2_ready, b + 1, rstd2_ready)
            for b in range(HALF // TPB, BATCHES):
                router_exponentials(b)

            def add_expert(step, k):
                _, h = PAIR_STEPS[k]
                pool.wait_ge(y_scaled, step + 1)
                acc = x1[:, h * HALF:(h + 1) * HALF, :].rearrange("p t d -> p (t d)")
                if not isinstance(step, int) or step >= 1:
                    pool.wait_ge(y_added, step)
                nc.gpsimd.tensor_tensor(acc, acc, y_sb[:, k % 2, :], ALU.add).then_inc(y_added, 1)

            for k in range(4):
                add_expert(k, k)
            with pool.Fori(1, PAIRS - 1) as i:
                for k in range(4):
                    add_expert(i * 4 + k, k)
            for k in range(3):
                add_expert((PAIRS - 1) * 4 + k, k)

        @block.scalar
        def _(act):
            act.dma_start(att_sb[:], att_w).then_inc(att_in, 16)
            act.wait_ge(pad_ready, 1)
            nc.scalar.activation(neg_max[:, 0:1], inv_sum[:, 0:1], ACT.Exp)

            def evict_q(j):
                t0, n = PREP[j]
                act.wait_ge(q_done, j + 1)
                act.wait_ge(bq_scaled, 1)
                nc.scalar.activation(qT[:, t0 * P:(t0 + n) * P], M[:, 0:n * P], ACT.Identity, bias=bqs_sb[:],
                                     scale=SCALE).then_inc(q_copied, 1)

            def copy_xT(j):
                t0, n = PREP[j]
                act.wait_ge(xT_done, j + 1)
                nc.scalar.activation(xT[:, t0 * P:(t0 + n) * P], M[:, 0:n * P], ACT.Copy).then_inc(xT_copied, 1)

            def split_g(j):
                t0, n = PREP[j]
                act.wait_ge(g_done, j + 1)
                nc.scalar.activation(g_hi[:, t0 * P:(t0 + n) * P], M[:, 0:n * P], ACT.Copy).then_inc(g_hi_ready, 1)

            def split_ctx(b, g):
                t0, n = CTX_GROUPS[g]
                bank, before_it = T_USE["ctx", b, g]
                w = min(n * P, KEYS - t0 * P)
                act.wait_ge(t_done[bank], before_it + 1)
                nc.scalar.activation(ct_hi[b % 2][:, t0 * P:t0 * P + w], T[bank][:, 0:w], ACT.Copy).then_inc(ct_hi_ready, 1)

            def exponentials(b, q):
                n = b * TPB + q
                act.wait_ge(clipped, n + 1)
                act.wait_ge(negmax_ready, n + 1)
                nc.scalar.activation(pr[:, b % 2, q, 0:KEYS], sc[:, q, 0:KEYS], ACT.Exp, bias=neg_max[:, n:n + 1],
                                     accum_out=row_sum[:, n:n + 1]).then_inc(p_ready, 1)

            def copy_pT(b, g):
                t0, n = PT_GROUPS[g]
                bank, before_it = T_USE["pt", b, g]
                rows = P if t0 < KT_FULL else K_REST
                act.wait_ge(t_done[bank], before_it + 1)
                nc.scalar.activation(pT[0:rows, t0:t0 + n, :].rearrange("p t q -> p (t q)"), T[bank][0:rows, 0:n * TPB * P],
                                     ACT.Copy).then_inc(t_free[bank], 1)

            def copy_oT(b):
                act.wait_ge(o_done, b + 1)
                nc.scalar.activation(oT[:], O[:, 0:TPB * P], ACT.Copy).then_inc(oT_copied, 1)

            def split_x2(b):
                act.wait_ge(x2_done, b + 1)
                nc.scalar.activation(x2_hi[:, b * QUERIES:(b + 1) * QUERIES], M[:, 0:QUERIES], ACT.Copy).then_inc(x2_hi_ready, 1)

            copy_xT(0)
            split_ctx(0, 0)
            evict_q(0)
            split_ctx(0, 1)
            split_g(0)
            split_ctx(0, 2)
            split_ctx(0, 3)
            split_ctx(1, 0)
            split_ctx(1, 1)
            for b in range(BATCHES):
                if b + 1 < len(PREP):
                    copy_xT(b + 1)
                if b >= 1:
                    for g in range(4):
                        copy_pT(b - 1, g)
                    exponentials(b, 0)
                if b >= 2:
                    split_x2(b - 2)
                if b + 1 < len(PREP):
                    evict_q(b + 1)
                if b + 1 < BATCHES:
                    split_ctx(b + 1, 2)
                    split_ctx(b + 1, 3)
                if b == 0:
                    exponentials(b, 0)
                if b + 1 < len(PREP):
                    split_g(b + 1)
                if b >= 1:
                    for g in range(4, len(PT_GROUPS)):
                        copy_pT(b - 1, g)
                if b == 0:
                    split_ctx(2, 0)
                    split_ctx(2, 1)
                exponentials(b, 1)
                if b >= 1:
                    copy_oT(b - 1)
                    if b + 2 < BATCHES:
                        split_ctx(b + 2, 0)
                        split_ctx(b + 2, 1)
            last = BATCHES - 1
            act.wait_ge(ldiff_ready, HALF // TPB)
            nc.scalar.activation(ex[:, 0:HALF, :], logit[:, 0:HALF, :], ACT.Exp).then_inc(exp_ready, 1)

            def ups(step, k, col, ih):
                act.wait_ge(gu_done, step * 4 + 2 * ih + 2)
                if not isinstance(step, int) or step >= 2:
                    act.wait_ge(act_ready, step * 2 - 2)
                nc.scalar.activation(up[:, k % 2, ih, :], S[2 * ih + 1][:], ACT.Identity,
                                     bias=gub1_sb[:, bass.ds(col + 2 + ih, 1)]).then_inc(up_copied, 1)

            def silus(step, k, ih):
                act.wait_ge(gate_copied, step * 2 + ih + 1)
                nc.scalar.activation(gate[:, k % 2, ih, :], gate[:, k % 2, ih, :], ACT.Silu,
                                     scale=ALPHA).then_inc(silu_ready, 1)

            def expert(step, k, col):
                for ih in range(2):
                    ups(step, k, col, ih)
                    silus(step, k, ih)

            def scale_y(step, k, e):
                _, h = PAIR_STEPS[k]
                act.wait_ge(y_done, step + 1)
                if not isinstance(step, int) or step >= 2:
                    act.wait_ge(y_added, step - 1)
                for t in range(HALF):
                    n = h * HALF + t
                    ins = nc.scalar.activation(y_sb[:, k % 2, t * DIM:(t + 1) * DIM], T[k % 2][:, t * DIM:(t + 1) * DIM],
                                               ACT.Copy, scale=w_scaled[:, bass.ds(e * TILES + n, 1)])
                ins.then_inc(y_scaled, 1)

            for g in range(3):
                copy_pT(last, g)
            act.wait_ge(gub1_ready, 1)
            ups(0, 0, 0, 0)
            copy_pT(last, 3)
            ups(0, 0, 0, 1)
            copy_pT(last, 4)
            split_x2(last - 1)
            copy_pT(last, 5)
            copy_pT(last, 6)
            copy_oT(last)
            for ih in range(2):
                silus(0, 0, ih)
            for ih in range(2):
                ups(1, 1, 4, ih)
            split_x2(last)
            for ih in range(2):
                silus(1, 1, ih)
            for k in range(4):
                e, h = PAIR_STEPS[k]
                act.wait_ge(route_ready, h + 1)
                scale_y(k, k, e)
                s = k + 2
                expert(s, s % 4, (s // 4 * 2 + PAIR_STEPS[s % 4][0]) * 4)
            with act.Fori(1, PAIRS - 1) as i:
                for k in range(4):
                    scale_y(i * 4 + k, k, i * 2 + PAIR_STEPS[k][0])
                    s = k + 2
                    expert(i * 4 + s, s % 4, i * 8 + (s // 4 * 2 + PAIR_STEPS[s % 4][0]) * 4)
            i = PAIRS - 1
            for k in range(4):
                if k < 3:
                    scale_y(i * 4 + k, k, i * 2 + PAIR_STEPS[k][0])
                s = k + 2
                if s < 4:
                    expert(i * 4 + s, s, (i * 2 + PAIR_STEPS[s][0]) * 4)
                if k == 0:
                    for h, bank in enumerate((O, M)):
                        act.wait_ge(wT_done, h + 1)
                        nc.scalar.activation(wT[:, h * HTOK:(h + 1) * HTOK], bank[0:EXPERTS, :], ACT.Copy).then_inc(wT_copied, 1)

        @block.vector
        def _(dve):
            links = [0]

            def link(ins):
                links[0] += 1
                ins.then_inc(chain, 1)
                dve.wait_ge(chain, links[0])

            def moments(src, st, m, v, t0, n, then):
                for t in range(t0, t0 + n):
                    ins = nc.vector.bn_stats(st[:, t, :], src[:, t, :])
                link(ins)
                for t in range(t0, t0 + n):
                    ins = nc.vector.bn_aggr(m[:, t, :], st[:, t, :])
                link(ins)
                nc.vector.tensor_scalar(v[:, t0:t0 + n], m[:, t0:t0 + n, 1], EPS, None, ALU.add).then_inc(then, 1)

            def normalise(dst, src, m, r, t0, n, ready, k, then):
                dve.wait_ge(ready, k)
                for t in range(t0, t0 + n):
                    ins = nc.vector.tensor_scalar(dst[:, t, :], src[:, t, :], m[:, t, 0:1], r[:, t:t + 1],
                                                  ALU.subtract, ALU.mult)
                ins.then_inc(then, 1)

            def split_g(j):
                t0, n = PREP[j]
                s = slice(t0 * P, (t0 + n) * P)
                dve.wait_ge(g_hi_ready, j + 1)
                nc.vector.tensor_tensor(g_lo[:, s], M[:, 0:n * P], g_hi[:, s].bitcast(F32), ALU.subtract)
                nc.vector.tensor_scalar(clip_hi[:, t0:t0 + n], M[:, 3 * P:3 * P + n], -1.0, CLIP, ALU.mult, ALU.add)
                nc.vector.tensor_scalar(row_max[:, t0:t0 + n, NCH], M[:, 3 * P:3 * P + n], -1.0, -CLIP,
                                        ALU.mult, ALU.add).then_inc(g_lo_ready, 1)

            def split_ctx(b, g):
                t0, n = CTX_GROUPS[g]
                bank, _ = T_USE["ctx", b, g]
                w = min(n * P, KEYS - t0 * P)
                s = slice(t0 * P, t0 * P + w)
                dve.wait_ge(ct_hi_ready, b * len(CTX_GROUPS) + g + 1)
                nc.vector.tensor_tensor(ct_lo[b % 2][:, s], T[bank][:, 0:w], ct_hi[b % 2][:, s].bitcast(F32),
                                        ALU.subtract).then_inc(t_free[bank], 1)

            def clip_scores(b, q, chunks, between):
                n = b * TPB + q
                if chunks[0] == 0:
                    dve.wait_ge(g_lo_ready, prep_of(n) + 1)
                    if b >= 1:
                        dve.wait_ge(p_ready, n - TPB + 1)
                for c in chunks:
                    c0, w, _ = SCORE_CHUNKS[c]
                    dve.wait_ge(s_done, n * NCH + c + 1)
                    nc.vector.tensor_scalar(sc[:, q, c0:c0 + w], S[c][:, 0:w], clip_hi[:, n:n + 1], None, ALU.min, ALU.max,
                                            accum_out=row_max[:, n, c:c + 1]).then_inc(s_free, 1)
                if chunks[-1] == NCH - 1:
                    between()
                    dve.wait_ge(s_free, (n + 1) * NCH)
                    nc.vector.tensor_reduce(neg_max[:, n:n + 1], row_max[:, n, :], AX.X, ALU.max, negate=True).then_inc(negmax_ready, 1)
                    nc.vector.tensor_scalar(sc[:, q, 0:KEYS], sc[:, q, 0:KEYS], row_max[:, n, NCH:NCH + 1], None,
                                            ALU.max).then_inc(clipped, 1)

            def residual(b):
                s = slice(b * TPB, (b + 1) * TPB)
                dve.wait_ge(p_ready, (b + 1) * TPB)
                link(nc.vector.reciprocal(inv_sum[:, s], row_sum[:, s]))
                dve.wait_ge(v_done, b + 1)
                dve.wait_ge(xb_ready, 1)
                for q in range(TPB):
                    n = b * TPB + q
                    ins = nc.vector.scalar_tensor_tensor(x1[:, n, :], O[:, q * DIM:(q + 1) * DIM], inv_sum[:, n:n + 1],
                                                         xb[:, n, :], ALU.mult, ALU.add)
                ins.then_inc(x1_ready, 1)

            def residual_moments(b):
                dve.wait_ge(x1_ready, b + 1)
                moments(x1, stats2, mv2, ve2, b * TPB, TPB, var2_ready)

            def split_x2(b):
                s = slice(b * QUERIES, (b + 1) * QUERIES)
                dve.wait_ge(x2_hi_ready, b + 1)
                nc.vector.tensor_tensor(x2_lo[:, s], M[:, 0:QUERIES], x2_hi[:, s].bitcast(F32),
                                        ALU.subtract).then_inc(x2_lo_ready, 1)

            def add_router_bias(b):
                s = slice(b * TPB, (b + 1) * TPB)
                dve.wait_ge(r_done, b + 1)
                dve.wait_ge(rows_in, 16)
                nc.vector.tensor_tensor(logit[:, s, :], M[:, 0:TPB * EXPERTS].rearrange("p (t e) -> p t e", e=EXPERTS),
                                        rb_sb.unsqueeze(1).to_broadcast([P, TPB, EXPERTS]), ALU.add).then_inc(logit_ready, 1)

            def route_differences(b):
                s = slice(b * TPB, (b + 1) * TPB)
                dve.wait_ge(logit_ready, b + 1)
                link(nc.vector.tensor_reduce(lmax[:, s], logit[:, s, :], AX.X, ALU.max))
                nc.vector.tensor_tensor(logit[:, s, :], logit[:, s, :],
                                        lmax[:, s].unsqueeze(2).to_broadcast([P, TPB, EXPERTS]),
                                        ALU.subtract).then_inc(ldiff_ready, 1)

            def half(h):
                return slice(h * HALF, (h + 1) * HALF)

            def route_probabilities(h):
                s = half(h)
                dve.wait_ge(exp_ready, 1 + 2 * h)
                link(nc.vector.tensor_reduce(esum[:, s], ex[:, s, :], AX.X, ALU.add))
                link(nc.vector.reciprocal(esum[:, s], esum[:, s]))
                nc.vector.tensor_tensor(prob[:, s, :], ex[:, s, :], esum[:, s].unsqueeze(2).to_broadcast([P, HALF, EXPERTS]),
                                        ALU.mult).then_inc(prob_ready, 1)

            def route_compare(h):
                s = half(h)
                cube = [P, HALF, EXPERTS, EXPERTS]
                b4 = beats[:].rearrange("p (t e) j -> p t e j", e=EXPERTS)
                t4 = ties[:].rearrange("p (t e) j -> p t e j", e=EXPERTS)
                other, own = prob[:, s, :].unsqueeze(2).to_broadcast(cube), prob[:, s, :].unsqueeze(3).to_broadcast(cube)
                dve.wait_ge(const_ready, SETUP_CONSTS)
                dve.wait_ge(prob_ready, h + 1)
                link(nc.vector.tensor_tensor(t4, other, own, ALU.is_equal))
                nc.vector.tensor_tensor(b4, other, own, ALU.is_gt)
                link(nc.vector.tensor_tensor(t4, t4, before[:].unsqueeze(1).to_broadcast(cube), ALU.mult))
                nc.vector.tensor_tensor(beats[:], beats[:], ties[:], ALU.add).then_inc(beats_ready, 1)

            def route_weights(h):
                s = half(h)
                dve.wait_ge(beats_ready, h + 1)
                link(nc.vector.tensor_reduce(rank[:, s, :], beats[:].rearrange("p (t e) j -> p t e j", e=EXPERTS), AX.X, ALU.add))
                link(nc.vector.scalar_tensor_tensor(w_route[:, s, :], rank[:, s, :], float(TOP_K), prob[:, s, :],
                                                    ALU.is_lt, ALU.mult))
                nc.vector.tensor_scalar(w_scaled[:].rearrange("p (e t) -> p t e", t=TILES)[:, s, :], w_route[:, s, :],
                                        1.0 / ALPHA, None, ALU.mult).then_inc(route_ready, 1)

            def split_w(e, buf):
                src = gu_sb[:, bass.ds(e * (2 * HIDDEN), 2 * HIDDEN)]
                nc.vector.tensor_copy(w_hi[buf][:], src).then_inc(w_hi_ready, 1)
                dve.wait_ge(w_hi_ready, e + 1)
                nc.vector.tensor_tensor(w_lo[buf][:], src, w_hi[buf][:].bitcast(F32), ALU.subtract).then_inc(w_ready, 1)

            def prep_of(n):
                return next(j for j, (t0, m) in enumerate(PREP) if t0 <= n < t0 + m)

            for i in range(2):
                nc.vector.memset(ct_hi[i][:, KEYS:KEYS_EVEN].bitcast(F32), 0.0)
                ins = nc.vector.memset(ct_lo[i][:, KEYS:KEYS_EVEN].bitcast(F32), 0.0)
            nc.vector.memset(inv_sum[:, 0:1], 0.0).then_inc(pad_ready, 1)
            dve.wait_ge(x0_in, 16)
            moments(x_sb, stats, mv, ve, 0, TPB, var_ready)
            normalise(xn, x_sb, mv, rstd, 0, TPB, rstd_ready, 1, xn_ready)
            dve.wait_ge(att_in, 16)
            nc.vector.tensor_scalar(bqs_sb[:], bqk_sb[:, 0:1], SCALE, None, ALU.mult).then_inc(bq_scaled, 1)
            split_ctx(0, 0)
            split_ctx(0, 1)
            split_g(0)
            split_ctx(0, 2)
            split_ctx(0, 3)
            dve.wait_ge(x1_in, 16)
            moments(x_sb, stats, mv, ve, *PREP[1], var_ready)
            for b in range(BATCHES):
                if b + 1 < BATCHES:
                    split_ctx(b + 1, 0)
                    split_ctx(b + 1, 1)

                def after_first():
                    if b >= 2:
                        residual(b - 2)
                        residual_moments(b - 2)

                def after_second():
                    if b + 1 < len(PREP):
                        split_g(b + 1)
                    if b >= 2:
                        add_router_bias(b - 2)

                if b == 0:
                    normalise(xn, x_sb, mv, rstd, *PREP[1], rstd_ready, 2, xn_ready)
                clip_scores(b, 0, range(NCH), after_first)
                if b == 0:
                    moments(x_sb, stats, mv, ve, *PREP[2], var_ready)
                if b >= 2:
                    normalise(xn2, x1, mv2, rstd2, (b - 2) * TPB, TPB, rstd2_ready, b - 1, xn2_ready)
                if b + 1 < BATCHES:
                    split_ctx(b + 1, 2)
                    split_ctx(b + 1, 3)
                if b >= 2:
                    split_x2(b - 2)
                clip_scores(b, 1, range(NCH), after_second)
                if b == 0:
                    normalise(xn, x_sb, mv, rstd, *PREP[2], rstd_ready, 3, xn_ready)
                    dve.wait_ge(more_in, 16)
                    nc.vector.tensor_scalar(gub1_sb[:], gub_sb, 1.0, None, ALU.add).then_inc(gub1_ready, 1)
                    link(nc.vector.tensor_copy(wr_hi[:], wr_sb))
                    nc.vector.tensor_tensor(wr_lo[:], wr_sb, wr_hi[:].bitcast(F32), ALU.subtract)
                if b == 1:
                    dve.wait_ge(gu_in, 16)
                    split_w(0, 0)
                    split_w(1, 1)
                if b >= 2:
                    route_differences(b - 2)
            last = BATCHES - 1

            def gates(step, k, col, ih):
                dve.wait_ge(gu_done, step * 4 + 2 * ih + 1)
                nc.vector.tensor_scalar(gate[:, k % 2, ih, :], S[2 * ih][:], gub_sb[:, bass.ds(col + ih, 1)], LIMIT,
                                        ALU.add, ALU.min).then_inc(gate_copied, 1)

            def clip_ups(step, k, ih):
                dve.wait_ge(up_copied, step * 2 + ih + 1)
                nc.vector.tensor_scalar(up[:, k % 2, ih, :], up[:, k % 2, ih, :], 1.0 + LIMIT, 1.0 - LIMIT,
                                        ALU.min, ALU.max).then_inc(up_clipped, 1)

            def products(step, k, halves=range(2)):
                for ih in halves:
                    dve.wait_ge(up_clipped, step * 2 + ih + 1)
                    dve.wait_ge(silu_ready, step * 2 + ih + 1)
                    if not isinstance(step, int) or step >= 2:
                        dve.wait_ge(y_done, step - 1)
                    nc.vector.tensor_tensor(act_t[k % 2][:, ih, :], up[:, k % 2, ih, :], gate[:, k % 2, ih, :],
                                            ALU.mult).then_inc(act_ready, 1)

            def expert(step, k, col, split=None):
                for ih in range(2):
                    gates(step, k, col, ih)
                    clip_ups(step, k, ih)
                if split is not None:
                    dve.wait_ge(gu_done, step * 4 + 4)
                    split_w(split, k % 2)
                products(step, k)

            residual(last - 1)
            residual_moments(last - 1)
            gates(0, 0, 0, 0)
            normalise(xn2, x1, mv2, rstd2, (last - 1) * TPB, TPB, rstd2_ready, last, xn2_ready)
            gates(0, 0, 0, 1)
            route_probabilities(0)
            route_compare(0)
            route_weights(0)
            for ih in range(2):
                clip_ups(0, 0, ih)
            split_x2(last - 1)
            add_router_bias(last - 1)
            route_differences(last - 1)
            residual(last)
            residual_moments(last)
            products(0, 0, [0])
            normalise(xn2, x1, mv2, rstd2, last * TPB, TPB, rstd2_ready, BATCHES, xn2_ready)
            products(0, 0, [1])
            for ih in range(2):
                gates(1, 1, 4, ih)
            split_x2(last)
            for ih in range(2):
                clip_ups(1, 1, ih)
            products(1, 1, [0])
            add_router_bias(last)
            route_differences(last)
            products(1, 1, [1])
            expert(2, 2, 0, split=2)
            route_probabilities(1)
            gates(3, 3, 4, 0)
            route_compare(1)
            clip_ups(3, 3, 0)
            gates(3, 3, 4, 1)
            clip_ups(3, 3, 1)
            route_weights(1)
            products(3, 3)
            dve.wait_ge(gu_done, 16)
            split_w(3, 1)
            with dve.Fori(1, PAIRS - 1) as i:
                for k in range(4):
                    e, h = PAIR_STEPS[k]
                    expert(i * 4 + k, k, i * 8 + e * 4, split=i * 2 + 2 + e if h == 1 else None)
            i = PAIRS - 1
            for k in range(4):
                expert(i * 4 + k, k, i * 8 + PAIR_STEPS[k][0] * 4)
            for h, bank in enumerate((O, M)):
                dve.wait_ge(db_done, h + 1)
                dve.wait_ge(y_added, STEPS - 2 + h)
                s = slice(h * HALF, (h + 1) * HALF)
                dst = out_sb if h == 0 else x1
                nc.vector.tensor_tensor(dst[:, s, :], bank[:].rearrange("p (t d) -> p t d", d=DIM), x1[:, s, :],
                                        ALU.add).then_inc(out_ready if h == 0 else bias_added, 1)
            dve.wait_ge(bias_added, 1)
            for t in range(HALF):
                n = HALF + t
                dve.wait_ge(y_tile_done, t + 1)
                w = (EXPERTS - 1) * TILES + n
                nc.vector.scalar_tensor_tensor(out_sb[:, n, :], S[t][:, 0:DIM], w_scaled[:, w:w + 1],
                                               x1[:, n, :], ALU.mult, ALU.add).then_inc(out_ready, 1)

        @block.tensor
        def _(pe):
            def three(dst, a_hi, a_lo, b_hi, b_lo):
                nc.tensor.matmul(dst, a_hi, b_hi, start=True, stop=False)
                nc.tensor.matmul(dst, a_hi, b_lo, start=False, stop=False)
                return nc.tensor.matmul(dst, a_lo, b_hi, start=False, stop=True)

            def transpose_xn(j):
                t0, n = PREP[j]
                if j == 0:
                    pe.wait_ge(const_ready, 3)
                else:
                    pe.wait_ge(g_lo_ready, j)
                pe.wait_ge(xn_ready, j + 1)
                for t in range(n):
                    ins = nc.tensor.transpose(M[:, t * P:(t + 1) * P], xn[:, t0 + t, :], ident[:])
                ins.then_inc(xT_done, 1)

            def project_q(j):
                t0, n = PREP[j]
                pe.wait_ge(att_in, 16)
                pe.wait_ge(xT_copied, j + 1)
                nc.tensor.matmul(M[:, 0:n * P], wq_sb, xT[:, t0 * P:(t0 + n) * P], start=True, stop=True).then_inc(q_done, 1)

            def fold_keys(j):
                t0, n = PREP[j]
                pe.wait_ge(q_copied, j + 1)
                nc.tensor.matmul(M[:, 0:n * P], wkT_sb, qT[:, t0 * P:(t0 + n) * P], start=True, stop=True)
                for t in range(n):
                    ins = nc.tensor.matmul(M[:, 3 * P + t:3 * P + t + 1], qT[:, (t0 + t) * P:(t0 + t + 1) * P],
                                           bqk_sb[:, 1:2], start=True, stop=True)
                ins.then_inc(g_done, 1)

            def transpose_ctx(b, g):
                t0, n = CTX_GROUPS[g]
                bank, before_it = T_USE["ctx", b, g]
                pe.wait_ge(ctx_in_s[b], 32)
                if before_it:
                    pe.wait_ge(t_free[bank], before_it)
                for t in range(t0, t0 + n):
                    rows = P if t < KT_FULL else K_REST
                    ins = nc.tensor.transpose(T[bank][:, (t - t0) * P:(t - t0) * P + rows], ctx_sb[b][0:rows, t, :],
                                              ident[0:rows, 0:rows])
                ins.then_inc(t_done[bank], 1)

            def scores(b, q, chunks):
                n = b * TPB + q
                tok = slice(n * P, (n + 1) * P)
                if q == 0 and chunks[0] == 0:
                    for bank in range(2):
                        g = len(CTX_GROUPS) - 2 + bank
                        pe.wait_ge(t_free[bank], T_USE["ctx", b, g][1] + 1)
                    pe.wait_ge(pad_ready, 1)
                if chunks[0] == 0:
                    pe.wait_ge(g_lo_ready, next(j for j, (t0, m) in enumerate(PREP) if t0 <= n < t0 + m) + 1)
                for c in chunks:
                    c0, _, w = SCORE_CHUNKS[c]
                    if n:
                        pe.wait_ge(s_free, (n - 1) * NCH + c + 1)
                    three(S[c][:, 0:w], g_hi[:, tok], g_lo[:, tok], ct_hi[b % 2][:, c0:c0 + w],
                          ct_lo[b % 2][:, c0:c0 + w]).then_inc(s_done, 1)

            def transpose_p(b, g):
                t0, n = PT_GROUPS[g]
                bank, before_it = T_USE["pt", b, g]
                pe.wait_ge(p_ready, (b + 1) * TPB)
                pe.wait_ge(t_free[bank], before_it)
                for t in range(t0, t0 + n):
                    rows = P if t < KT_FULL else K_REST
                    for q in range(TPB):
                        at = ((t - t0) * TPB + q) * P
                        ins = nc.tensor.transpose(T[bank][0:rows, at:at + P], pr[:, b % 2, q, t * P:t * P + rows], ident[:])
                ins.then_inc(t_done[bank], 1)

            def weighted_sum(b, g):
                t0, n = PT_GROUPS[g]
                bank, before_it = T_USE["pt", b, g]
                pe.wait_ge(t_free[bank], before_it + 1)
                if g == 0 and b:
                    pe.wait_ge(x1_ready, b)
                for t in range(t0, t0 + n):
                    rows = P if t < KT_FULL else K_REST
                    ins = nc.tensor.matmul(O[:, 0:TPB * P], ctx_sb[b][0:rows, t, :], pT[0:rows, t, :],
                                           start=(t == 0), stop=(t == KT - 1))
                if t == KT - 1:
                    ins.then_inc(o_done, 1)

            def project_v(b):
                pe.wait_ge(more_in, 16)
                pe.wait_ge(oT_copied, b + 1)
                for q in range(TPB):
                    ins = nc.tensor.matmul(O[:, q * DIM:(q + 1) * DIM], oT[:, q * P:(q + 1) * P], wv_sb, start=True, stop=True)
                ins.then_inc(v_done, 1)

            def transpose_x2(b):
                pe.wait_ge(xn2_ready, b + 1)
                if b:
                    pe.wait_ge(logit_ready, b)
                for q in range(TPB):
                    ins = nc.tensor.transpose(M[:, q * P:(q + 1) * P], xn2[:, b * TPB + q, :], ident[:])
                ins.then_inc(x2_done, 1)

            def router(b):
                pe.wait_ge(x2_lo_ready, b + 1)
                for q in range(TPB):
                    tok = slice((b * TPB + q) * P, (b * TPB + q + 1) * P)
                    ins = three(M[:, q * EXPERTS:(q + 1) * EXPERTS], x2_hi[:, tok], x2_lo[:, tok], wr_hi[:], wr_lo[:])
                ins.then_inc(r_done, 1)

            pe.wait_ge(const_ready, 3)
            for _ in range(WARM_UP):
                nc.tensor.matmul(S[0][:, 0:P], ident[:], ident[:], start=True, stop=True)
            transpose_xn(0)
            transpose_ctx(0, 0)
            project_q(0)
            transpose_ctx(0, 1)
            fold_keys(0)
            transpose_ctx(0, 2)
            transpose_ctx(0, 3)

            def sum_part(b, part):
                for g in range(3) if part == 0 else range(3, len(PT_GROUPS)):
                    if part == 1 and g + 1 < len(PT_GROUPS):
                        transpose_p(b, g + 1)
                    weighted_sum(b, g)
                    if part == 0 and g < 2:
                        transpose_p(b, g + 2)

            for b in range(BATCHES):
                if b + 1 < BATCHES:
                    transpose_ctx(b + 1, 0)
                    transpose_ctx(b + 1, 1)
                scores(b, 0, [0, 1])
                if b >= 2:
                    project_v(b - 2)
                scores(b, 0, [2])
                if b >= 2:
                    transpose_p(b - 1, 0)
                    transpose_p(b - 1, 1)
                scores(b, 0, [3])
                if b + 1 < len(PREP):
                    transpose_xn(b + 1)
                if b == 1:
                    transpose_p(0, 0)
                    transpose_p(0, 1)
                if b >= 1:
                    sum_part(b - 1, 0)
                if b >= 2:
                    transpose_x2(b - 2)
                if b + 1 < len(PREP):
                    project_q(b + 1)
                if b + 1 < BATCHES:
                    transpose_ctx(b + 1, 2)
                    transpose_ctx(b + 1, 3)
                scores(b, 1, range(NCH))
                if b + 1 < len(PREP):
                    fold_keys(b + 1)
                if b >= 2:
                    router(b - 2)
                if b >= 1:
                    sum_part(b - 1, 1)
            last = BATCHES - 1

            def gate_up(step, k, ih, loads):
                _, h = PAIR_STEPS[k]
                tok = slice(h * HTOK, (h + 1) * HTOK)
                buf = k % 2
                if ih == 0:
                    pe.wait_ge(w_ready, loads)
                for part in range(2):
                    if isinstance(step, int) and step == 0:
                        if ih == 0 and part == 0:
                            pe.wait_ge(s_free, TILES * NCH)
                    else:
                        pe.wait_ge(up_copied if part else gate_copied, step * 2 + ih - 1)
                    col = slice((part * 2 + ih) * P, (part * 2 + ih + 1) * P)
                    three(S[2 * ih + part][:], w_hi[buf][:, col], w_lo[buf][:, col], x2_hi[:, tok], x2_lo[:, tok]).then_inc(gu_done, 1)

            def down(step, k, e, tiles_apart=False):
                if isinstance(step, int) and step < 2:
                    pe.wait_ge(t_free[k % 2], T_TOTAL[k % 2])
                else:
                    pe.wait_ge(y_scaled, step - 1)
                for t in range(HALF):
                    for ih in range(2):
                        if t == 0:
                            pe.wait_ge(act_ready, step * 2 + ih + 1)
                        dst = S[t][:, 0:DIM] if tiles_apart else T[k % 2][:, t * DIM:(t + 1) * DIM]
                        ins = nc.tensor.matmul(dst, act_t[k % 2][:, ih, t * P:(t + 1) * P],
                                               dn_sb[:, bass.ds((e * 2 + ih) * DIM, DIM)], start=(ih == 0), stop=(ih == 1))
                    if tiles_apart:
                        ins.then_inc(y_tile_done, 1)
                if not tiles_apart:
                    ins.then_inc(y_done, 1)

            gate_up(0, 0, 0, 1)
            gate_up(0, 0, 1, 1)
            project_v(last - 1)
            transpose_p(last, 0)
            transpose_p(last, 1)
            sum_part(last, 0)
            transpose_x2(last - 1)
            sum_part(last, 1)
            router(last - 1)
            project_v(last)
            gate_up(1, 1, 0, 2)
            gate_up(1, 1, 1, 2)
            transpose_x2(last)
            pe.wait_ge(dn_in, 16)
            for k in range(4):
                down(k, k, PAIR_STEPS[k][0])
                if k == 0:
                    router(last)
                s = k + 2
                for ih in range(2):
                    gate_up(s, s % 4, ih, s // 4 * 2 + PAIR_STEPS[s % 4][0] + 1)
            with pe.Fori(1, PAIRS - 1) as i:
                for k in range(4):
                    down(i * 4 + k, k, i * 2 + PAIR_STEPS[k][0])
                    s = k + 2
                    for ih in range(2):
                        gate_up(i * 4 + s, s % 4, ih, i * 2 + s // 4 * 2 + PAIR_STEPS[s % 4][0] + 1)
            i = PAIRS - 1
            for k in range(4):
                down(i * 4 + k, k, i * 2 + PAIR_STEPS[k][0], tiles_apart=(k == 3))
                s = k + 2
                if s < 4:
                    for ih in range(2):
                        gate_up(i * 4 + s, s, ih, i * 2 + PAIR_STEPS[s][0] + 1)
                if k == 0:
                    pe.wait_ge(logit_ready, BATCHES)
                    pe.wait_ge(route_ready, 2)
                    for h, bank in enumerate((O, M)):
                        for t in range(HALF):
                            ins = nc.tensor.transpose(bank[0:EXPERTS, t * P:(t + 1) * P], w_route[:, h * HALF + t, :], ident[:])
                        ins.then_inc(wT_done, 1)
                if k == 1:
                    pe.wait_ge(db_in, 16)
                    for h, bank in enumerate((O, M)):
                        pe.wait_ge(wT_copied, h + 1)
                        for t in range(HALF):
                            n = h * HALF + t
                            ins = nc.tensor.matmul(bank[:, t * DIM:(t + 1) * DIM], wT[:, n * P:(n + 1) * P], db_sb[:],
                                                   start=True, stop=True)
                        ins.then_inc(db_done, 1)


def kernel(x, ctx_1024, L0_xattn_Wq, L0_xattn_bq, L0_xattn_Wk, L0_xattn_bk, L0_xattn_Wv, L0_xattn_bv,
           L0_ffn_router_weight, L0_ffn_router_bias, L0_ffn_gate_up_proj, L0_ffn_gate_up_bias,
           L0_ffn_down_proj, L0_ffn_down_bias):
    import concourse.bacc as bacc
    from concourse.bass_utils import run_bass_kernel_spmd

    a = np.ascontiguousarray
    arrays = {
        "in_x": a(x), "in_ctx": a(ctx_1024),
        "in_att_w": a(np.concatenate([L0_xattn_Wq, np.asarray(L0_xattn_Wk).T, np.asarray(L0_xattn_bq)[:, None],
                                      np.asarray(L0_xattn_bk)[:, None]], axis=1)),
        "in_more_w": a(np.concatenate([L0_xattn_Wv, np.asarray(L0_ffn_router_weight).T,
                                       np.asarray(L0_ffn_gate_up_bias).reshape(EXPERTS * 4, P).T], axis=1)),
        "in_rows": a(np.concatenate([L0_xattn_bv, L0_ffn_router_bias])),
        "in_gu": a(L0_ffn_gate_up_proj), "in_dn": a(L0_ffn_down_proj), "in_db": a(L0_ffn_down_bias),
    }
    nc = bacc.Bacc("TRN2", target_bir_lowering=False, num_devices=1)
    args = [nc.dram_tensor(n, v.shape, mybir.dt.from_np(v.dtype), kind="ExternalInput").ap() for n, v in arrays.items()]
    out = nc.dram_tensor("out_x", (BATCHES, QUERIES, DIM), F32, kind="ExternalOutput").ap()
    build(nc, *args, out)
    r = run_bass_kernel_spmd(nc, [arrays], core_ids=[0])
    return r.results[0]["out_x"]
```

```python
import numpy as np
import concourse.bass as bass
from concourse import mybir
from contextlib import ExitStack

F32 = mybir.dt.float32
F32R = mybir.dt.float32r
ALU = mybir.AluOpType
ACT = mybir.ActivationFunctionType
AX = mybir.AxisListType

BATCHES, QUERIES, DIM = 4, 256, 128
KEYS = 1601
EXPERTS, HIDDEN, TOP_K = 8, 256, 2
P = 128
TILES = BATCHES * QUERIES // P
TPB = QUERIES // P
KT_FULL = KEYS // P
KT = KT_FULL + 1
K_REST = KEYS - KT_FULL * P
KEYS_EVEN = KEYS + KEYS % 2
SCALE = float(1.0 / np.sqrt(DIM).astype(np.float32))
CLIP = 100.0
EPS = 1e-5
ALPHA, LIMIT = 1.702, 7.0
E_BASE = float(np.float32(np.e))

_CW = KEYS // 4 // 2 * 2
SCORE_CHUNKS = [(c * _CW, _CW, _CW) for c in range(3)] + [(3 * _CW, KEYS - 3 * _CW, KEYS_EVEN - 3 * _CW)]
NCH = len(SCORE_CHUNKS)
PREP = [(0, 2), (2, 3), (5, 3)]
CTX_GROUPS = [(t, min(4, KT - t)) for t in range(0, KT, 4)]
PT_GROUPS = [(t, min(2, KT - t)) for t in range(0, KT, 2)]
CTX_FIRST = 4
PAIRS = EXPERTS // 2
WARM_UP = 10
HALF = TILES // 2
HTOK = HALF * P
STEPS = 2 * EXPERTS
PAIR_STEPS = [(0, 0), (1, 0), (0, 1), (1, 1)]


def _transpose_bank_uses():
    order = [("ctx", 0, g) for g in range(len(CTX_GROUPS))]
    for b in range(BATCHES + 1):
        for ctx_part, pt_part in (((0, 1), (0, 1, 2, 3)), ((2, 3), (4, 5, 6))):
            order += [("ctx", b + 1, g) for g in ctx_part if b + 1 < BATCHES]
            order += [("pt", b - 1, g) for g in pt_part if b >= 1]
    seen, found = [0, 0], {}
    for kind, b, g in order:
        found[kind, b, g] = (g % 2, seen[g % 2])
        seen[g % 2] += 1
    return found, seen


T_USE, T_TOTAL = _transpose_bank_uses()


def build(nc, x, ctx_in, att_w, more_w, rows, gu, dn, db, out):
    es = ExitStack()
    with es:
        def sb(name, shape, dt=F32):
            return es.enter_context(nc.sbuf_tensor(name, shape, dt))

        def sem(name):
            return es.enter_context(nc.semaphore(name))

        x_sb = sb("x_sb", [P, TILES, DIM])
        ctx_sb = [sb(f"ctx_sb{b}", [P, KT, DIM]) for b in range(BATCHES)]
        att_sb = sb("att_sb", [P, 2 * DIM + 2])
        wq_sb, wkT_sb, bqk_sb = att_sb[:, 0:DIM], att_sb[:, DIM:2 * DIM], att_sb[:, 2 * DIM:2 * DIM + 2]
        more_sb = sb("more_sb", [P, DIM + EXPERTS + EXPERTS * 4])
        wv_sb, wr_sb, gub_sb = more_sb[:, 0:DIM], more_sb[:, DIM:DIM + EXPERTS], more_sb[:, DIM + EXPERTS:]
        rows_sb = sb("rows_sb", [P, DIM + EXPERTS])
        bv_sb, rb_sb = rows_sb[:, 0:DIM], rows_sb[:, DIM:DIM + EXPERTS]
        bqs_sb = sb("bqs_sb", [P, 1])
        gu_sb = sb("gu_sb", [P, EXPERTS * 2 * HIDDEN])
        gub1_sb = sb("gub1_sb", [P, EXPERTS * 4])
        dn_sb = sb("dn_sb", [P, EXPERTS * 2 * DIM])
        db_sb = sb("db_sb", [EXPERTS, DIM])
        ident = sb("ident", [P, P])
        before = sb("before", [P, EXPERTS, EXPERTS])
        minus_half = sb("minus_half", [P, TILES])
        e_base = sb("e_base", [P, TPB * EXPERTS])
        stats = sb("stats", [P, TILES, 6])
        mv = sb("mv", [P, TILES, 2])
        ve = sb("ve", [P, TILES])
        rstd = sb("rstd", [P, TILES])
        neg_mean = sb("neg_mean", [P, TILES])
        shift = sb("shift", [P, TILES])
        xn = sb("xn", [P, TILES, DIM])
        stats2 = sb("stats2", [P, TILES, 6])
        mv2 = sb("mv2", [P, TILES, 2])
        ve2 = sb("ve2", [P, TILES])
        rstd2 = sb("rstd2", [P, TILES])
        xn2 = sb("xn2", [P, TILES, DIM])
        xT = sb("xT", [P, TILES * P])
        qT = sb("qT", [P, TILES * P])
        g_hi = sb("g_hi", [P, TILES * P], F32R)
        g_lo = sb("g_lo", [P, TILES * P], F32R)
        clip_hi = sb("clip_hi", [P, TILES])
        row_max = sb("row_max", [P, TILES, NCH + 1])
        neg_max = sb("neg_max", [P, TILES])
        row_sum = sb("row_sum", [P, TILES])
        inv_sum = sb("inv_sum", [P, TILES])
        ct_hi = [sb(f"ct_hi{i}", [P, KEYS_EVEN], F32R) for i in range(2)]
        ct_lo = [sb(f"ct_lo{i}", [P, KEYS_EVEN], F32R) for i in range(2)]
        sc = sb("sc", [P, TPB, KEYS_EVEN])
        pr = sb("pr", [P, 2, TPB, KEYS_EVEN])
        pT = sb("pT", [P, KT, TPB * P])
        oT = sb("oT", [P, TPB * P])
        xb = sb("xb", [P, TILES, DIM])
        x1 = sb("x1", [P, TILES, DIM])
        x2_hi = sb("x2_hi", [P, TILES * P], F32R)
        x2_lo = sb("x2_lo", [P, TILES * P], F32R)
        wr_hi = sb("wr_hi", [P, EXPERTS], F32R)
        wr_lo = sb("wr_lo", [P, EXPERTS], F32R)
        logit = sb("logit", [P, TILES, EXPERTS])
        lmax = sb("lmax", [P, TILES])
        ex = sb("ex", [P, TILES, EXPERTS])
        esum = sb("esum", [P, TILES])
        esum_inv = sb("esum_inv", [P, TILES])
        prob = sb("prob", [P, TILES, EXPERTS])
        beats = sb("beats", [P, HALF * EXPERTS, EXPERTS])
        ties = sb("ties", [P, HALF * EXPERTS, EXPERTS])
        rank = sb("rank", [P, TILES, EXPERTS])
        w_route = sb("w_route", [P, TILES, EXPERTS])
        w_scaled = sb("w_scaled", [P, TILES * EXPERTS])
        wT = sb("wT", [EXPERTS, TILES * P])
        w_hi = [sb(f"w_hi{i}", [P, 2 * HIDDEN], F32R) for i in range(2)]
        w_lo = [sb(f"w_lo{i}", [P, 2 * HIDDEN], F32R) for i in range(2)]
        gate = sb("gate", [P, 2, 2, HTOK])
        up = sb("up", [P, 2, 2, HTOK])
        act_t = [old[:].rearrange("p (c t) -> p c t", c=2) for old in (xT, qT)]
        y_sb = xn2[:].rearrange("p (k t) d -> p k (t d)", k=2)
        out_sb = xn

        S = [es.enter_context(nc.psum_tensor(f"S{i}", [P, 512], F32)) for i in range(4)]
        T = [es.enter_context(nc.psum_tensor(f"T{i}", [P, 512], F32)) for i in range(2)]
        O = es.enter_context(nc.psum_tensor("O", [P, 512], F32))
        M = es.enter_context(nc.psum_tensor("M", [P, 512], F32))
        BIAS = (O, M)

        bq_scaled = sem("bq_scaled")
        x0_in, x1_in, att_in, more_in = sem("x0_in"), sem("x1_in"), sem("att_in"), sem("more_in")
        ctx_in_s = [sem(f"ctx_in{b}") for b in range(BATCHES)]
        ctx_first_in = sem("ctx_first_in")
        rows_in, db_in, gu_in, dn_in, out_done = sem("rows_in"), sem("db_in"), sem("gu_in"), sem("dn_in"), sem("out_done")
        const_ready = sem("const_ready")
        pad_ready = sem("pad_ready")
        blank_ready = sem("blank_ready")
        var_ready, rstd_ready, xn_ready = sem("var_ready"), sem("rstd_ready"), sem("xn_ready")
        shift_ready = sem("shift_ready")
        stats2_ready, mv2_ready = sem("stats2_ready"), sem("mv2_ready")
        var2_ready, rstd2_ready, xn2_ready = sem("var2_ready"), sem("rstd2_ready"), sem("xn2_ready")
        xT_done, xT_copied, q_done, q_copied = sem("xT_done"), sem("xT_copied"), sem("q_done"), sem("q_copied")
        g_done, g_hi_ready, g_lo_ready = sem("g_done"), sem("g_hi_ready"), sem("g_lo_ready")
        t_done, t_free = [sem("t_done0"), sem("t_done1")], [sem("t_free0"), sem("t_free1")]
        ct_hi_ready = sem("ct_hi_ready")
        s_done, s_free = sem("s_done"), sem("s_free")
        negmax_ready, clipped, p_ready = sem("negmax_ready"), sem("clipped"), sem("p_ready")
        o_done, oT_copied, v_done, x1_ready = sem("o_done"), sem("oT_copied"), sem("v_done"), sem("x1_ready")
        xb_ready, inv_ready = sem("xb_ready"), sem("inv_ready")
        x2_done, x2_hi_ready, x2_lo_ready = sem("x2_done"), sem("x2_hi_ready"), sem("x2_lo_ready")
        r_done, logit_ready, ldiff_ready, exp_ready = sem("r_done"), sem("logit_ready"), sem("ldiff_ready"), sem("exp_ready")
        lmax_ready, esum_ready, esum_inv_ready = sem("lmax_ready"), sem("esum_ready"), sem("esum_inv_ready")
        prob_ready, beats_ready, route_ready = sem("prob_ready"), sem("beats_ready"), sem("route_ready")
        chain = sem("chain")
        w_ready = sem("w_ready")
        w_hi_ready = sem("w_hi_ready")
        gub1_ready = sem("gub1_ready")
        gu_done, gate_copied, up_copied = sem("gu_done"), sem("gate_copied"), sem("up_copied")
        silu_ready, up_clipped, act_ready = sem("silu_ready"), sem("up_clipped"), sem("act_ready")
        y_done, y_scaled, y_added = sem("y_done"), sem("y_scaled"), sem("y_added")
        bias_added, y_tile_added, y_tile_done = sem("bias_added"), sem("y_tile_added"), sem("y_tile_done")
        wT_done, wT_copied, db_done = sem("wT_done"), sem("wT_copied"), sem("db_done")
        first_half_ready, out_ready = sem("first_half_ready"), sem("out_ready")

        block = es.enter_context(nc.Block())

        x_v = x.rearrange("b (t p) d -> p (b t) d", p=P)
        out_v = out.rearrange("b (t p) d -> p (b t) d", p=P)
        SETUP_CONSTS = 6

        @block.sync
        def _(sp):
            sp.dma_start(x_sb[:, 0:TPB], x_v[:, 0:TPB]).then_inc(x0_in, 16)
            sp.dma_start(x_sb[:, TPB:TILES], x_v[:, TPB:TILES]).then_inc(x1_in, 16)
            for b in range(BATCHES):
                full = ctx_in[b, 0:KT_FULL * P, :].rearrange("(p t) d -> p t d", t=KT_FULL)
                if b == 0:
                    sp.dma_start(ctx_sb[b][:, 0:CTX_FIRST, :], full[:, 0:CTX_FIRST, :]).then_inc(ctx_first_in, 16)
                    full = full[:, CTX_FIRST:, :]
                sp.dma_start(ctx_sb[b][:, KT_FULL - full.shape[1]:KT_FULL, :], full).then_inc(ctx_in_s[b], 16)
                sp.dma_start(ctx_sb[b][0:K_REST, KT_FULL, :], ctx_in[b, KT_FULL * P:KEYS, :]).then_inc(ctx_in_s[b], 16)
                if b == 0:
                    sp.dma_start(rows_sb[:], rows.partition_broadcast(P)).then_inc(rows_in, 16)
                    sp.dma_start(more_sb[:], more_w).then_inc(more_in, 16)
            sp.dma_start(gu_sb[:].rearrange("p (e n) -> p e n", e=EXPERTS), gu.rearrange("e h n -> h e n")).then_inc(gu_in, 16)
            sp.dma_start(dn_sb[:].rearrange("p (e c h) -> p e c h", e=EXPERTS, c=2),
                         dn.rearrange("e (c p) h -> p e c h", p=P)).then_inc(dn_in, 16)
            sp.dma_start(db_sb[:], db).then_inc(db_in, 16)
            sp.wait_ge(first_half_ready, 1)
            sp.dma_start(out_v[:, 0:HALF], out_sb[:, 0:HALF]).then_inc(out_done, 16)
            for t in range(HALF, TILES, 2):
                sp.wait_ge(out_ready, t - HALF + 2)
                sp.dma_start(out_v[:, t:t + 2], out_sb[:, t:t + 2]).then_inc(out_done, 16)
            sp.wait_ge(out_done, 48)

        @block.gpsimd
        def _(pool):
            nc.gpsimd.memset(ident[:], 0.0).then_inc(const_ready, 1)
            nc.gpsimd.memset(minus_half[:], -0.5).then_inc(const_ready, 1)
            pool.wait_ge(const_ready, 2)
            nc.gpsimd.affine_select(out=ident[:], in_=ident[:], compare_op=ALU.not_equal, fill=1.0, base=0,
                                    pattern=[[-1, P]], channel_multiplier=1).then_inc(const_ready, 1)

            def inverse_root(dst, src, n, ready, k, then):
                pool.wait_ge(ready, k)
                nc.gpsimd.tensor_tensor(dst, src, minus_half[:, 0:n], ALU.pow).then_inc(then, 1)

            inverse_root(rstd[:, 0:TPB], ve[:, 0:TPB], TPB, var_ready, 1, rstd_ready)
            for j in range(1, len(PREP)):
                t0, n = PREP[j]
                inverse_root(rstd[:, t0:t0 + n], ve[:, t0:t0 + n], n, var_ready, j + 1, rstd_ready)
                pool.wait_ge(rstd_ready, j + 1)
                nc.gpsimd.tensor_tensor(shift[:, t0:t0 + n], neg_mean[:, t0:t0 + n], rstd[:, t0:t0 + n],
                                        ALU.mult).then_inc(shift_ready, 1)
            nc.gpsimd.memset(e_base[:], E_BASE).then_inc(const_ready, 1)
            nc.gpsimd.memset(before[:], 1.0).then_inc(const_ready, 1)
            pool.wait_ge(const_ready, 5)
            nc.gpsimd.affine_select(out=before[:], in_=before[:], compare_op=ALU.is_gt, fill=0.0, base=0,
                                    pattern=[[1, EXPERTS], [-1, EXPERTS]], channel_multiplier=0).then_inc(const_ready, 1)
            pool.wait_ge(rows_in, 16)
            nc.gpsimd.tensor_tensor(xb[:], x_sb[:], bv_sb.unsqueeze(1).to_broadcast([P, TILES, DIM]),
                                    ALU.add).then_inc(xb_ready, 1)

            def router_exponentials(b):
                s = slice(b * TPB, (b + 1) * TPB)
                pool.wait_ge(ldiff_ready, b + 1)
                nc.gpsimd.tensor_tensor(ex[:, s, :], e_base[:].rearrange("p (t e) -> p t e", e=EXPERTS),
                                        logit[:, s, :], ALU.pow).then_inc(exp_ready, 1)

            for b in range(BATCHES):
                s = slice(b * TPB, (b + 1) * TPB)
                inverse_root(rstd2[:, s], ve2[:, s], TPB, var2_ready, b + 1, rstd2_ready)
            for b in range(HALF // TPB, BATCHES):
                router_exponentials(b)

            def add_expert(step, k):
                _, h = PAIR_STEPS[k]
                pool.wait_ge(y_scaled, step + 1)
                acc = x1[:, h * HALF:(h + 1) * HALF, :].rearrange("p t d -> p (t d)")
                if not isinstance(step, int) or step >= 1:
                    pool.wait_ge(y_added, step)
                nc.gpsimd.tensor_tensor(acc, acc, y_sb[:, k % 2, :], ALU.add).then_inc(y_added, 1)

            for k in range(4):
                add_expert(k, k)
            with pool.Fori(1, PAIRS - 1) as i:
                for k in range(4):
                    add_expert(i * 4 + k, k)
            add_expert((PAIRS - 1) * 4, 0)
            pool.wait_ge(y_scaled, STEPS - 2)
            pool.wait_ge(bias_added, 1)
            nc.gpsimd.tensor_tensor(out_sb[:, 0:HALF, :].rearrange("p t d -> p (t d)"),
                                    x1[:, 0:HALF, :].rearrange("p t d -> p (t d)"), y_sb[:, 1, :],
                                    ALU.add).then_inc(first_half_ready, 1)

        @block.scalar
        def _(act):
            act.dma_start(att_sb[:], att_w).then_inc(att_in, 16)
            act.wait_ge(pad_ready, 1)
            nc.scalar.activation(neg_max[:, 0:1], inv_sum[:, 0:1], ACT.Exp)

            def evict_q(j):
                t0, n = PREP[j]
                act.wait_ge(q_done, j + 1)
                act.wait_ge(bq_scaled, 1)
                nc.scalar.activation(qT[:, t0 * P:(t0 + n) * P], M[:, 0:n * P], ACT.Identity, bias=bqs_sb[:],
                                     scale=SCALE).then_inc(q_copied, 1)

            def normalise(j):
                t0, n = PREP[j]
                act.wait_ge(shift_ready, j)
                for t in range(t0, t0 + n):
                    ins = nc.scalar.activation(xn[:, t, :], x_sb[:, t, :], ACT.Identity, bias=shift[:, t:t + 1],
                                               scale=rstd[:, t:t + 1])
                ins.then_inc(xn_ready, 1)

            def copy_xT(j):
                t0, n = PREP[j]
                act.wait_ge(xT_done, j + 1)
                nc.scalar.activation(xT[:, t0 * P:(t0 + n) * P], M[:, 0:n * P], ACT.Copy).then_inc(xT_copied, 1)

            def split_g(j):
                t0, n = PREP[j]
                act.wait_ge(g_done, j + 1)
                nc.scalar.activation(g_hi[:, t0 * P:(t0 + n) * P], M[:, 0:n * P], ACT.Copy).then_inc(g_hi_ready, 1)

            def split_ctx(b, g):
                t0, n = CTX_GROUPS[g]
                bank, before_it = T_USE["ctx", b, g]
                w = min(n * P, KEYS - t0 * P)
                act.wait_ge(t_done[bank], before_it + 1)
                nc.scalar.activation(ct_hi[b % 2][:, t0 * P:t0 * P + w], T[bank][:, 0:w], ACT.Copy).then_inc(ct_hi_ready, 1)

            def exponentials(b, q):
                n = b * TPB + q
                act.wait_ge(clipped, n + 1)
                act.wait_ge(negmax_ready, n + 1)
                nc.scalar.activation(pr[:, b % 2, q, 0:KEYS], sc[:, q, 0:KEYS], ACT.Exp, bias=neg_max[:, n:n + 1],
                                     accum_out=row_sum[:, n:n + 1]).then_inc(p_ready, 1)

            def copy_pT(b, g):
                t0, n = PT_GROUPS[g]
                bank, before_it = T_USE["pt", b, g]
                rows = P if t0 < KT_FULL else K_REST
                act.wait_ge(t_done[bank], before_it + 1)
                nc.scalar.activation(pT[0:rows, t0:t0 + n, :].rearrange("p t q -> p (t q)"), T[bank][0:rows, 0:n * TPB * P],
                                     ACT.Copy).then_inc(t_free[bank], 1)

            def copy_oT(b):
                act.wait_ge(o_done, b + 1)
                nc.scalar.activation(oT[:], O[:, 0:TPB * P], ACT.Copy).then_inc(oT_copied, 1)

            def split_x2(b):
                act.wait_ge(x2_done, b + 1)
                nc.scalar.activation(x2_hi[:, b * QUERIES:(b + 1) * QUERIES], M[:, 0:QUERIES], ACT.Copy).then_inc(x2_hi_ready, 1)

            copy_xT(0)
            split_ctx(0, 0)
            evict_q(0)
            split_ctx(0, 1)
            split_g(0)
            split_ctx(0, 2)
            split_ctx(0, 3)
            normalise(1)
            normalise(2)
            copy_xT(1)
            split_ctx(1, 0)
            split_ctx(1, 1)
            evict_q(1)
            exponentials(0, 0)
            split_ctx(1, 2)
            split_ctx(1, 3)
            split_g(1)
            split_ctx(2, 0)
            split_ctx(2, 1)
            exponentials(0, 1)
            for b in range(1, BATCHES):
                if b + 1 < len(PREP):
                    copy_xT(b + 1)
                for g in range(4):
                    copy_pT(b - 1, g)
                if b + 1 < len(PREP):
                    evict_q(b + 1)
                if b + 1 < BATCHES:
                    split_ctx(b + 1, 2)
                    split_ctx(b + 1, 3)
                if b >= 2:
                    split_x2(b - 2)
                exponentials(b, 0)
                if b + 1 < len(PREP):
                    split_g(b + 1)
                for g in range(4, len(PT_GROUPS)):
                    copy_pT(b - 1, g)
                exponentials(b, 1)
                copy_oT(b - 1)
                if b + 2 < BATCHES:
                    split_ctx(b + 2, 0)
                    split_ctx(b + 2, 1)
            last = BATCHES - 1
            act.wait_ge(ldiff_ready, HALF // TPB)
            nc.scalar.activation(ex[:, 0:HALF, :], logit[:, 0:HALF, :], ACT.Exp).then_inc(exp_ready, 1)

            def ups(step, k, col, ih):
                act.wait_ge(gu_done, step * 4 + 2 * ih + 2)
                if not isinstance(step, int) or step >= 2:
                    act.wait_ge(act_ready, step * 2 - 2)
                nc.scalar.activation(up[:, k % 2, ih, :], S[2 * ih + 1][:], ACT.Identity,
                                     bias=gub1_sb[:, bass.ds(col + 2 + ih, 1)]).then_inc(up_copied, 1)

            def silus(step, k, ih):
                act.wait_ge(gate_copied, step * 2 + ih + 1)
                nc.scalar.activation(gate[:, k % 2, ih, :], gate[:, k % 2, ih, :], ACT.Silu,
                                     scale=ALPHA).then_inc(silu_ready, 1)

            def expert(step, k, col):
                for ih in range(2):
                    ups(step, k, col, ih)
                    silus(step, k, ih)

            def split_w_hi(step, k, e):
                act.wait_ge(gu_done, step * 4 + 4)
                nc.scalar.activation(w_hi[k % 2][:], gu_sb[:, bass.ds(e * (2 * HIDDEN), 2 * HIDDEN)],
                                     ACT.Copy).then_inc(w_hi_ready, 1)

            def copy_wT(h):
                act.wait_ge(wT_done, h + 1)
                nc.scalar.activation(wT[:, h * HTOK:(h + 1) * HTOK], BIAS[h][0:EXPERTS, :], ACT.Copy).then_inc(wT_copied, 1)

            def scale_y(step, k, e):
                _, h = PAIR_STEPS[k]
                act.wait_ge(y_done, step + 1)
                if not isinstance(step, int) or step >= 2:
                    act.wait_ge(y_added, step - 1)
                for t in range(HALF):
                    n = h * HALF + t
                    ins = nc.scalar.activation(y_sb[:, k % 2, t * DIM:(t + 1) * DIM], T[k % 2][:, t * DIM:(t + 1) * DIM],
                                               ACT.Copy, scale=w_scaled[:, bass.ds(e * TILES + n, 1)])
                ins.then_inc(y_scaled, 1)

            for g in range(3):
                copy_pT(last, g)
            act.wait_ge(gub1_ready, 1)
            ups(0, 0, 0, 0)
            copy_pT(last, 3)
            ups(0, 0, 0, 1)
            copy_pT(last, 4)
            split_x2(last - 1)
            copy_pT(last, 5)
            copy_pT(last, 6)
            copy_oT(last)
            for ih in range(2):
                silus(0, 0, ih)
            for ih in range(2):
                ups(1, 1, 4, ih)
            copy_wT(0)
            split_x2(last)
            for ih in range(2):
                silus(1, 1, ih)
            for k in range(4):
                e, h = PAIR_STEPS[k]
                act.wait_ge(route_ready, h + 1)
                scale_y(k, k, e)
                s = k + 2
                e, h = PAIR_STEPS[s % 4]
                expert(s, s % 4, (s // 4 * 2 + e) * 4)
                if h == 1:
                    split_w_hi(s, s, 2 + e)
            with act.Fori(1, PAIRS - 1) as i:
                for k in range(4):
                    scale_y(i * 4 + k, k, i * 2 + PAIR_STEPS[k][0])
                    s = k + 2
                    e, h = PAIR_STEPS[s % 4]
                    expert(i * 4 + s, s % 4, i * 8 + (s // 4 * 2 + e) * 4)
                    if h == 1:
                        split_w_hi(i * 4 + s, s, i * 2 + 2 + e)
            i = PAIRS - 1
            for k in range(4):
                if k < 2:
                    scale_y(i * 4 + k, k, i * 2 + PAIR_STEPS[k][0])
                if k == 0:
                    copy_wT(1)
                s = k + 2
                if s < 4:
                    expert(i * 4 + s, s, (i * 2 + PAIR_STEPS[s][0]) * 4)

        @block.vector
        def _(dve):
            links = [0]

            def link(ins):
                links[0] += 1
                ins.then_inc(chain, 1)
                dve.wait_ge(chain, links[0])

            def moments(src, st, m, v, t0, n, then, negated=None):
                for t in range(t0, t0 + n):
                    ins = nc.vector.bn_stats(st[:, t, :], src[:, t, :])
                link(ins)
                for t in range(t0, t0 + n):
                    ins = nc.vector.bn_aggr(m[:, t, :], st[:, t, :])
                link(ins)
                if negated is not None:
                    nc.vector.tensor_scalar(negated[:, t0:t0 + n], m[:, t0:t0 + n, 0], -1.0, None, ALU.mult)
                nc.vector.tensor_scalar(v[:, t0:t0 + n], m[:, t0:t0 + n, 1], EPS, None, ALU.add).then_inc(then, 1)

            def normalise(dst, src, m, r, t0, n, ready, k, then):
                dve.wait_ge(ready, k)
                for t in range(t0, t0 + n):
                    ins = nc.vector.tensor_scalar(dst[:, t, :], src[:, t, :], m[:, t, 0:1], r[:, t:t + 1],
                                                  ALU.subtract, ALU.mult)
                ins.then_inc(then, 1)

            def split_g(j):
                t0, n = PREP[j]
                s = slice(t0 * P, (t0 + n) * P)
                dve.wait_ge(g_hi_ready, j + 1)
                nc.vector.tensor_tensor(g_lo[:, s], M[:, 0:n * P], g_hi[:, s].bitcast(F32), ALU.subtract)
                nc.vector.tensor_scalar(clip_hi[:, t0:t0 + n], M[:, 3 * P:3 * P + n], -1.0, CLIP, ALU.mult, ALU.add)
                nc.vector.tensor_scalar(row_max[:, t0:t0 + n, NCH], M[:, 3 * P:3 * P + n], -1.0, -CLIP,
                                        ALU.mult, ALU.add).then_inc(g_lo_ready, 1)

            def split_ctx(b, g):
                t0, n = CTX_GROUPS[g]
                bank, _ = T_USE["ctx", b, g]
                w = min(n * P, KEYS - t0 * P)
                s = slice(t0 * P, t0 * P + w)
                dve.wait_ge(ct_hi_ready, b * len(CTX_GROUPS) + g + 1)
                nc.vector.tensor_tensor(ct_lo[b % 2][:, s], T[bank][:, 0:w], ct_hi[b % 2][:, s].bitcast(F32),
                                        ALU.subtract).then_inc(t_free[bank], 1)

            def clip_scores(b, q, chunks=range(NCH)):
                n = b * TPB + q
                if chunks[0] == 0:
                    dve.wait_ge(g_lo_ready, prep_of(n) + 1)
                    if b >= 1:
                        dve.wait_ge(p_ready, n - TPB + 1)
                for c in chunks:
                    c0, w, _ = SCORE_CHUNKS[c]
                    dve.wait_ge(s_done, n * NCH + c + 1)
                    nc.vector.tensor_scalar(sc[:, q, c0:c0 + w], S[c][:, 0:w], clip_hi[:, n:n + 1], None, ALU.min, ALU.max,
                                            accum_out=row_max[:, n, c:c + 1]).then_inc(s_free, 1)

            def finish_scores(b, q, between=None):
                n = b * TPB + q
                dve.wait_ge(s_free, (n + 1) * NCH)
                nc.vector.tensor_reduce(neg_max[:, n:n + 1], row_max[:, n, :], AX.X, ALU.max, negate=True).then_inc(negmax_ready, 1)
                if between:
                    between()
                nc.vector.tensor_scalar(sc[:, q, 0:KEYS], sc[:, q, 0:KEYS], row_max[:, n, NCH:NCH + 1], None,
                                        ALU.max).then_inc(clipped, 1)

            def invert_sums(b):
                s = slice(b * TPB, (b + 1) * TPB)
                dve.wait_ge(p_ready, (b + 1) * TPB)
                nc.vector.reciprocal(inv_sum[:, s], row_sum[:, s]).then_inc(inv_ready, 1)

            def residual(b):
                dve.wait_ge(inv_ready, b + 1)
                dve.wait_ge(v_done, b + 1)
                dve.wait_ge(xb_ready, 1)
                for q in range(TPB):
                    n = b * TPB + q
                    ins = nc.vector.scalar_tensor_tensor(x1[:, n, :], O[:, q * DIM:(q + 1) * DIM], inv_sum[:, n:n + 1],
                                                         xb[:, n, :], ALU.mult, ALU.add)
                ins.then_inc(x1_ready, 1)

            def residual_stats(b):
                dve.wait_ge(x1_ready, b + 1)
                for n in range(b * TPB, (b + 1) * TPB):
                    ins = nc.vector.bn_stats(stats2[:, n, :], x1[:, n, :])
                ins.then_inc(stats2_ready, 1)

            def residual_mean(b):
                dve.wait_ge(stats2_ready, b + 1)
                for n in range(b * TPB, (b + 1) * TPB):
                    ins = nc.vector.bn_aggr(mv2[:, n, :], stats2[:, n, :])
                ins.then_inc(mv2_ready, 1)

            def residual_variance(b):
                s = slice(b * TPB, (b + 1) * TPB)
                dve.wait_ge(mv2_ready, b + 1)
                nc.vector.tensor_scalar(ve2[:, s], mv2[:, s, 1], EPS, None, ALU.add).then_inc(var2_ready, 1)

            def residual_moments(b):
                residual_stats(b)
                residual_mean(b)
                residual_variance(b)

            def split_x2(b):
                s = slice(b * QUERIES, (b + 1) * QUERIES)
                dve.wait_ge(x2_hi_ready, b + 1)
                nc.vector.tensor_tensor(x2_lo[:, s], M[:, 0:QUERIES], x2_hi[:, s].bitcast(F32),
                                        ALU.subtract).then_inc(x2_lo_ready, 1)

            def add_router_bias(b):
                s = slice(b * TPB, (b + 1) * TPB)
                dve.wait_ge(r_done, b + 1)
                dve.wait_ge(rows_in, 16)
                nc.vector.tensor_tensor(logit[:, s, :], M[:, 0:TPB * EXPERTS].rearrange("p (t e) -> p t e", e=EXPERTS),
                                        rb_sb.unsqueeze(1).to_broadcast([P, TPB, EXPERTS]), ALU.add).then_inc(logit_ready, 1)

            def logit_maximum(b):
                s = slice(b * TPB, (b + 1) * TPB)
                dve.wait_ge(logit_ready, b + 1)
                nc.vector.tensor_reduce(lmax[:, s], logit[:, s, :], AX.X, ALU.max).then_inc(lmax_ready, 1)

            def logit_differences(b):
                s = slice(b * TPB, (b + 1) * TPB)
                dve.wait_ge(lmax_ready, b + 1)
                nc.vector.tensor_tensor(logit[:, s, :], logit[:, s, :],
                                        lmax[:, s].unsqueeze(2).to_broadcast([P, TPB, EXPERTS]),
                                        ALU.subtract).then_inc(ldiff_ready, 1)

            def half(h):
                return slice(h * HALF, (h + 1) * HALF)

            def sum_exponentials(h):
                s = half(h)
                dve.wait_ge(exp_ready, 1 + 2 * h)
                nc.vector.tensor_reduce(esum[:, s], ex[:, s, :], AX.X, ALU.add).then_inc(esum_ready, 1)

            def invert_exponentials(h):
                s = half(h)
                dve.wait_ge(esum_ready, h + 1)
                nc.vector.reciprocal(esum_inv[:, s], esum[:, s]).then_inc(esum_inv_ready, 1)

            def route_probabilities(h):
                s = half(h)
                dve.wait_ge(esum_inv_ready, h + 1)
                nc.vector.tensor_tensor(prob[:, s, :], ex[:, s, :], esum_inv[:, s].unsqueeze(2).to_broadcast([P, HALF, EXPERTS]),
                                        ALU.mult).then_inc(prob_ready, 1)

            def route_compare(h):
                s = half(h)
                cube = [P, HALF, EXPERTS, EXPERTS]
                b4 = beats[:].rearrange("p (t e) j -> p t e j", e=EXPERTS)
                t4 = ties[:].rearrange("p (t e) j -> p t e j", e=EXPERTS)
                other, own = prob[:, s, :].unsqueeze(2).to_broadcast(cube), prob[:, s, :].unsqueeze(3).to_broadcast(cube)
                dve.wait_ge(const_ready, SETUP_CONSTS)
                dve.wait_ge(prob_ready, h + 1)
                link(nc.vector.tensor_tensor(t4, other, own, ALU.is_equal))
                nc.vector.tensor_tensor(b4, other, own, ALU.is_gt)
                link(nc.vector.tensor_tensor(t4, t4, before[:].unsqueeze(1).to_broadcast(cube), ALU.mult))
                nc.vector.tensor_tensor(beats[:], beats[:], ties[:], ALU.add).then_inc(beats_ready, 1)

            def route_weights(h):
                s = half(h)
                dve.wait_ge(beats_ready, h + 1)
                link(nc.vector.tensor_reduce(rank[:, s, :], beats[:].rearrange("p (t e) j -> p t e j", e=EXPERTS), AX.X, ALU.add))
                link(nc.vector.scalar_tensor_tensor(w_route[:, s, :], rank[:, s, :], float(TOP_K), prob[:, s, :],
                                                    ALU.is_lt, ALU.mult))
                nc.vector.tensor_scalar(w_scaled[:].rearrange("p (e t) -> p t e", t=TILES)[:, s, :], w_route[:, s, :],
                                        1.0 / ALPHA, None, ALU.mult).then_inc(route_ready, 1)

            def split_w_hi(e, buf):
                nc.vector.tensor_copy(w_hi[buf][:], gu_sb[:, bass.ds(e * (2 * HIDDEN), 2 * HIDDEN)]).then_inc(w_hi_ready, 1)

            def split_w_lo(e, buf):
                dve.wait_ge(w_hi_ready, e + 1)
                nc.vector.tensor_tensor(w_lo[buf][:], gu_sb[:, bass.ds(e * (2 * HIDDEN), 2 * HIDDEN)],
                                        w_hi[buf][:].bitcast(F32), ALU.subtract).then_inc(w_ready, 1)

            def prep_of(n):
                return next(j for j, (t0, m) in enumerate(PREP) if t0 <= n < t0 + m)

            nc.vector.memset(qT[:, 0:P], 0.0).then_inc(blank_ready, 1)
            for i in range(2):
                nc.vector.memset(ct_hi[i][:, KEYS:KEYS_EVEN].bitcast(F32), 0.0)
                ins = nc.vector.memset(ct_lo[i][:, KEYS:KEYS_EVEN].bitcast(F32), 0.0)
            nc.vector.memset(inv_sum[:, 0:1], 0.0).then_inc(pad_ready, 1)
            dve.wait_ge(x0_in, 16)
            moments(x_sb, stats, mv, ve, 0, TPB, var_ready)
            normalise(xn, x_sb, mv, rstd, 0, TPB, rstd_ready, 1, xn_ready)
            dve.wait_ge(att_in, 16)
            nc.vector.tensor_scalar(bqs_sb[:], bqk_sb[:, 0:1], SCALE, None, ALU.mult).then_inc(bq_scaled, 1)
            dve.wait_ge(x1_in, 16)
            for j in range(1, len(PREP)):
                t0, n = PREP[j]
                moments(x_sb, stats, mv, ve, t0, n, var_ready, neg_mean)
            split_ctx(0, 0)
            split_ctx(0, 1)
            split_g(0)
            split_ctx(0, 2)
            split_ctx(0, 3)
            clip_scores(0, 0)
            finish_scores(0, 0)
            split_ctx(1, 0)
            split_ctx(1, 1)
            clip_scores(0, 1)
            split_ctx(1, 2)
            split_ctx(1, 3)
            split_g(1)
            finish_scores(0, 1)
            for b in range(1, BATCHES):
                if b + 1 < BATCHES:
                    split_ctx(b + 1, 0)
                    split_ctx(b + 1, 1)
                if b >= 2:
                    invert_sums(b - 2)
                    chunks_before = 1 if b + 1 < BATCHES else 2
                    clip_scores(b, 0, range(chunks_before))
                    residual(b - 2)
                    clip_scores(b, 0, range(chunks_before, 3))
                    residual_stats(b - 2)
                    clip_scores(b, 0, [3])
                    residual_mean(b - 2)
                    finish_scores(b, 0, between=lambda: residual_variance(b - 2))
                    normalise(xn2, x1, mv2, rstd2, (b - 2) * TPB, TPB, rstd2_ready, b - 1, xn2_ready)
                else:
                    clip_scores(b, 0)
                    finish_scores(b, 0)
                    dve.wait_ge(more_in, 16)
                    nc.vector.tensor_scalar(gub1_sb[:], gub_sb, 1.0, None, ALU.add).then_inc(gub1_ready, 1)
                    link(nc.vector.tensor_copy(wr_hi[:], wr_sb))
                    nc.vector.tensor_tensor(wr_lo[:], wr_sb, wr_hi[:].bitcast(F32), ALU.subtract)
                if b + 1 < BATCHES:
                    split_ctx(b + 1, 2)
                    split_ctx(b + 1, 3)
                if b >= 2:
                    split_x2(b - 2)
                clip_scores(b, 1)
                if b + 1 < len(PREP):
                    split_g(b + 1)
                if b >= 2:
                    add_router_bias(b - 2)
                finish_scores(b, 1)
                if b == 1:
                    dve.wait_ge(gu_in, 16)
                    for e in range(2):
                        split_w_hi(e, e)
                        split_w_lo(e, e)
                if b >= 2:
                    logit_maximum(b - 2)
                    logit_differences(b - 2)
            last = BATCHES - 1

            def gates(step, k, col, ih):
                dve.wait_ge(gu_done, step * 4 + 2 * ih + 1)
                nc.vector.tensor_scalar(gate[:, k % 2, ih, :], S[2 * ih][:], gub_sb[:, bass.ds(col + ih, 1)], LIMIT,
                                        ALU.add, ALU.min).then_inc(gate_copied, 1)

            def clip_ups(step, k, ih):
                dve.wait_ge(up_copied, step * 2 + ih + 1)
                nc.vector.tensor_scalar(up[:, k % 2, ih, :], up[:, k % 2, ih, :], 1.0 + LIMIT, 1.0 - LIMIT,
                                        ALU.min, ALU.max).then_inc(up_clipped, 1)

            def products(step, k, halves=range(2)):
                for ih in halves:
                    dve.wait_ge(up_clipped, step * 2 + ih + 1)
                    dve.wait_ge(silu_ready, step * 2 + ih + 1)
                    if not isinstance(step, int) or step >= 2:
                        dve.wait_ge(y_done, step - 1)
                    nc.vector.tensor_tensor(act_t[k % 2][:, ih, :], up[:, k % 2, ih, :], gate[:, k % 2, ih, :],
                                            ALU.mult).then_inc(act_ready, 1)

            def expert(step, k, col, split=None):
                for ih in range(2):
                    gates(step, k, col, ih)
                    clip_ups(step, k, ih)
                products(step, k, [0])
                if split is not None:
                    split_w_lo(split, k % 2)
                products(step, k, [1])

            invert_sums(last - 1)
            residual(last - 1)
            residual_moments(last - 1)
            gates(0, 0, 0, 0)
            sum_exponentials(0)
            normalise(xn2, x1, mv2, rstd2, (last - 1) * TPB, TPB, rstd2_ready, last, xn2_ready)
            invert_exponentials(0)
            gates(0, 0, 0, 1)
            invert_sums(last)
            route_probabilities(0)
            clip_ups(0, 0, 0)
            route_compare(0)
            clip_ups(0, 0, 1)
            split_x2(last - 1)
            route_weights(0)
            add_router_bias(last - 1)
            residual(last)
            logit_maximum(last - 1)
            residual_stats(last)
            logit_differences(last - 1)
            residual_mean(last)
            residual_variance(last)
            products(0, 0, [0])
            normalise(xn2, x1, mv2, rstd2, last * TPB, TPB, rstd2_ready, BATCHES, xn2_ready)
            products(0, 0, [1])
            for ih in range(2):
                gates(1, 1, 4, ih)
            split_x2(last)
            for ih in range(2):
                clip_ups(1, 1, ih)
            products(1, 1, [0])
            add_router_bias(last)
            products(1, 1, [1])
            logit_maximum(last)
            gates(2, 2, 0, 0)
            logit_differences(last)
            clip_ups(2, 2, 0)
            gates(2, 2, 0, 1)
            clip_ups(2, 2, 1)
            products(2, 2, [0])
            split_w_lo(2, 0)
            sum_exponentials(1)
            products(2, 2, [1])
            invert_exponentials(1)
            gates(3, 3, 4, 0)
            route_probabilities(1)
            clip_ups(3, 3, 0)
            route_compare(1)
            gates(3, 3, 4, 1)
            clip_ups(3, 3, 1)
            products(3, 3)
            route_weights(1)
            split_w_lo(3, 1)
            with dve.Fori(1, PAIRS - 1) as i:
                for k in range(4):
                    e, h = PAIR_STEPS[k]
                    expert(i * 4 + k, k, i * 8 + e * 4, split=i * 2 + 2 + e if h == 1 else None)
            i = PAIRS - 1
            for k in range(3):
                expert(i * 4 + k, k, i * 8 + PAIR_STEPS[k][0] * 4)

            def add_bias(h):
                dve.wait_ge(db_done, h + 1)
                dve.wait_ge(y_added, STEPS - 3)
                s = slice(h * HALF, (h + 1) * HALF)
                nc.vector.tensor_tensor(x1[:, s, :], BIAS[h][:].rearrange("p (t d) -> p t d", d=DIM), x1[:, s, :],
                                        ALU.add).then_inc(bias_added, 1)

            col = i * 8 + 4
            add_bias(0)
            gates(STEPS - 1, 3, col, 0)
            add_bias(1)
            clip_ups(STEPS - 1, 3, 0)
            gates(STEPS - 1, 3, col, 1)
            products(STEPS - 1, 3, [0])
            clip_ups(STEPS - 1, 3, 1)
            products(STEPS - 1, 3, [1])
            dve.wait_ge(bias_added, 2)
            dve.wait_ge(y_done, STEPS - 1)
            for t in range(HALF):
                n = HALF + t
                w = (EXPERTS - 2) * TILES + n
                nc.vector.scalar_tensor_tensor(x1[:, n, :], T[0][:, t * DIM:(t + 1) * DIM], w_scaled[:, w:w + 1],
                                               x1[:, n, :], ALU.mult, ALU.add).then_inc(y_tile_added, 1)
            for t in range(HALF):
                n = HALF + t
                dve.wait_ge(y_tile_added, t + 1)
                dve.wait_ge(y_tile_done, t + 1)
                w = (EXPERTS - 1) * TILES + n
                nc.vector.scalar_tensor_tensor(out_sb[:, n, :], S[t][:, 0:DIM], w_scaled[:, w:w + 1],
                                               x1[:, n, :], ALU.mult, ALU.add).then_inc(out_ready, 1)

        @block.tensor
        def _(pe):
            def three(dst, a_hi, a_lo, b_hi, b_lo):
                nc.tensor.matmul(dst, a_hi, b_hi, start=True, stop=False)
                nc.tensor.matmul(dst, a_hi, b_lo, start=False, stop=False)
                return nc.tensor.matmul(dst, a_lo, b_hi, start=False, stop=True)

            def transpose_xn(j):
                t0, n = PREP[j]
                if j == 0:
                    pe.wait_ge(const_ready, 3)
                else:
                    pe.wait_ge(g_lo_ready, j)
                pe.wait_ge(xn_ready, j + 1)
                for t in range(n):
                    ins = nc.tensor.transpose(M[:, t * P:(t + 1) * P], xn[:, t0 + t, :], ident[:])
                ins.then_inc(xT_done, 1)

            def project_q(j):
                t0, n = PREP[j]
                pe.wait_ge(att_in, 16)
                pe.wait_ge(xT_copied, j + 1)
                nc.tensor.matmul(M[:, 0:n * P], wq_sb, xT[:, t0 * P:(t0 + n) * P], start=True, stop=True).then_inc(q_done, 1)

            def fold_keys(j):
                t0, n = PREP[j]
                pe.wait_ge(q_copied, j + 1)
                nc.tensor.matmul(M[:, 0:n * P], wkT_sb, qT[:, t0 * P:(t0 + n) * P], start=True, stop=True)
                for t in range(n):
                    ins = nc.tensor.matmul(M[:, 3 * P + t:3 * P + t + 1], qT[:, (t0 + t) * P:(t0 + t + 1) * P],
                                           bqk_sb[:, 1:2], start=True, stop=True)
                ins.then_inc(g_done, 1)

            def transpose_ctx(b, g):
                t0, n = CTX_GROUPS[g]
                bank, before_it = T_USE["ctx", b, g]
                if b == 0 and t0 + n <= CTX_FIRST:
                    pe.wait_ge(ctx_first_in, 16)
                else:
                    pe.wait_ge(ctx_in_s[b], 32)
                if before_it:
                    pe.wait_ge(t_free[bank], before_it)
                for t in range(t0, t0 + n):
                    rows = P if t < KT_FULL else K_REST
                    ins = nc.tensor.transpose(T[bank][:, (t - t0) * P:(t - t0) * P + rows], ctx_sb[b][0:rows, t, :],
                                              ident[0:rows, 0:rows])
                ins.then_inc(t_done[bank], 1)

            def scores(b, q, chunks):
                n = b * TPB + q
                tok = slice(n * P, (n + 1) * P)
                if n == 0 and chunks[0] == 0:
                    pe.wait_ge(pad_ready, 1)
                if chunks[0] == 0:
                    pe.wait_ge(g_lo_ready, next(j for j, (t0, m) in enumerate(PREP) if t0 <= n < t0 + m) + 1)
                for c in chunks:
                    c0, _, w = SCORE_CHUNKS[c]
                    if q == 0:
                        bank, before_it = T_USE["ctx", b, (c0 + w - 1) // P // CTX_GROUPS[0][1]]
                        pe.wait_ge(t_free[bank], before_it + 1)
                    if n:
                        pe.wait_ge(s_free, (n - 1) * NCH + c + 1)
                    three(S[c][:, 0:w], g_hi[:, tok], g_lo[:, tok], ct_hi[b % 2][:, c0:c0 + w],
                          ct_lo[b % 2][:, c0:c0 + w]).then_inc(s_done, 1)

            def transpose_p(b, g):
                t0, n = PT_GROUPS[g]
                bank, before_it = T_USE["pt", b, g]
                pe.wait_ge(p_ready, (b + 1) * TPB)
                pe.wait_ge(t_free[bank], before_it)
                for t in range(t0, t0 + n):
                    rows = P if t < KT_FULL else K_REST
                    for q in range(TPB):
                        at = ((t - t0) * TPB + q) * P
                        ins = nc.tensor.transpose(T[bank][0:rows, at:at + P], pr[:, b % 2, q, t * P:t * P + rows], ident[:])
                ins.then_inc(t_done[bank], 1)

            def weighted_sum(b, g):
                t0, n = PT_GROUPS[g]
                bank, before_it = T_USE["pt", b, g]
                pe.wait_ge(t_free[bank], before_it + 1)
                if g == 0 and b:
                    pe.wait_ge(x1_ready, b)
                for t in range(t0, t0 + n):
                    rows = P if t < KT_FULL else K_REST
                    ins = nc.tensor.matmul(O[:, 0:TPB * P], ctx_sb[b][0:rows, t, :], pT[0:rows, t, :],
                                           start=(t == 0), stop=(t == KT - 1))
                if t == KT - 1:
                    ins.then_inc(o_done, 1)

            def project_v(b):
                pe.wait_ge(more_in, 16)
                pe.wait_ge(oT_copied, b + 1)
                for q in range(TPB):
                    ins = nc.tensor.matmul(O[:, q * DIM:(q + 1) * DIM], oT[:, q * P:(q + 1) * P], wv_sb, start=True, stop=True)
                ins.then_inc(v_done, 1)

            def transpose_x2(b):
                pe.wait_ge(xn2_ready, b + 1)
                if b:
                    pe.wait_ge(logit_ready, b)
                for q in range(TPB):
                    ins = nc.tensor.transpose(M[:, q * P:(q + 1) * P], xn2[:, b * TPB + q, :], ident[:])
                ins.then_inc(x2_done, 1)

            def router(b):
                pe.wait_ge(x2_lo_ready, b + 1)
                for q in range(TPB):
                    tok = slice((b * TPB + q) * P, (b * TPB + q + 1) * P)
                    ins = three(M[:, q * EXPERTS:(q + 1) * EXPERTS], x2_hi[:, tok], x2_lo[:, tok], wr_hi[:], wr_lo[:])
                ins.then_inc(r_done, 1)

            pe.wait_ge(blank_ready, 1)
            for _ in range(WARM_UP):
                nc.tensor.matmul(S[0][:, 0:P], qT[:, 0:P], qT[:, 0:P], start=True, stop=True)
            transpose_xn(0)
            transpose_ctx(0, 0)
            project_q(0)
            transpose_ctx(0, 1)
            fold_keys(0)
            transpose_ctx(0, 2)
            transpose_ctx(0, 3)

            def sum_part(b, part):
                for g in range(3) if part == 0 else range(3, len(PT_GROUPS)):
                    if part == 1 and g + 1 < len(PT_GROUPS):
                        transpose_p(b, g + 1)
                    weighted_sum(b, g)
                    if part == 0 and g < 2:
                        transpose_p(b, g + 2)

            scores(0, 0, range(NCH))
            transpose_xn(1)
            transpose_ctx(1, 0)
            transpose_ctx(1, 1)
            project_q(1)
            scores(0, 1, range(NCH))
            transpose_ctx(1, 2)
            transpose_ctx(1, 3)
            fold_keys(1)
            for b in range(1, BATCHES):
                if b + 1 < BATCHES:
                    transpose_ctx(b + 1, 0)
                    transpose_ctx(b + 1, 1)
                scores(b, 0, [0, 1])
                if 2 <= b < BATCHES - 1:
                    project_v(b - 2)
                scores(b, 0, [2])
                if b == BATCHES - 1:
                    project_v(b - 2)
                if b >= 2:
                    transpose_p(b - 1, 0)
                    transpose_p(b - 1, 1)
                scores(b, 0, [3])
                if b + 1 < len(PREP):
                    transpose_xn(b + 1)
                if b == 1:
                    transpose_p(0, 0)
                    transpose_p(0, 1)
                sum_part(b - 1, 0)
                if b + 1 < len(PREP):
                    project_q(b + 1)
                if b + 1 < BATCHES:
                    transpose_ctx(b + 1, 2)
                    transpose_ctx(b + 1, 3)
                if b >= 2:
                    transpose_x2(b - 2)
                scores(b, 1, range(NCH))
                if b + 1 < len(PREP):
                    fold_keys(b + 1)
                if b >= 2:
                    router(b - 2)
                sum_part(b - 1, 1)
            last = BATCHES - 1

            def gate_up(step, k, ih, loads):
                _, h = PAIR_STEPS[k]
                tok = slice(h * HTOK, (h + 1) * HTOK)
                buf = k % 2
                if ih == 0:
                    pe.wait_ge(w_ready, loads)
                for part in range(2):
                    if isinstance(step, int) and step == 0:
                        if ih == 0 and part == 0:
                            pe.wait_ge(s_free, TILES * NCH)
                    else:
                        pe.wait_ge(up_copied if part else gate_copied, step * 2 + ih - 1)
                    col = slice((part * 2 + ih) * P, (part * 2 + ih + 1) * P)
                    three(S[2 * ih + part][:], w_hi[buf][:, col], w_lo[buf][:, col], x2_hi[:, tok], x2_lo[:, tok]).then_inc(gu_done, 1)

            def down(step, k, e, tiles_apart=False):
                if isinstance(step, int) and step < 2:
                    pe.wait_ge(t_free[k % 2], T_TOTAL[k % 2])
                else:
                    pe.wait_ge(y_scaled, step - 1)
                for t in range(HALF):
                    for ih in range(2):
                        if t == 0:
                            pe.wait_ge(act_ready, step * 2 + ih + 1)
                        dst = S[t][:, 0:DIM] if tiles_apart else T[k % 2][:, t * DIM:(t + 1) * DIM]
                        ins = nc.tensor.matmul(dst, act_t[k % 2][:, ih, t * P:(t + 1) * P],
                                               dn_sb[:, bass.ds((e * 2 + ih) * DIM, DIM)], start=(ih == 0), stop=(ih == 1))
                    if tiles_apart:
                        ins.then_inc(y_tile_done, 1)
                if not tiles_apart:
                    ins.then_inc(y_done, 1)

            def transpose_weights(h):
                pe.wait_ge(route_ready, h + 1)
                for t in range(HALF):
                    ins = nc.tensor.transpose(BIAS[h][0:EXPERTS, t * P:(t + 1) * P], w_route[:, h * HALF + t, :], ident[:])
                ins.then_inc(wT_done, 1)

            def routed_bias(h):
                pe.wait_ge(db_in, 16)
                pe.wait_ge(wT_copied, h + 1)
                for t in range(HALF):
                    n = h * HALF + t
                    ins = nc.tensor.matmul(BIAS[h][:, t * DIM:(t + 1) * DIM], wT[:, n * P:(n + 1) * P], db_sb[:],
                                           start=True, stop=True)
                ins.then_inc(db_done, 1)

            gate_up(0, 0, 0, 1)
            project_v(last - 1)
            transpose_p(last, 0)
            transpose_p(last, 1)
            gate_up(0, 0, 1, 1)
            sum_part(last, 0)
            transpose_x2(last - 1)
            sum_part(last, 1)
            router(last - 1)
            project_v(last)
            gate_up(1, 1, 0, 2)
            gate_up(1, 1, 1, 2)
            pe.wait_ge(x1_ready, BATCHES)
            transpose_weights(0)
            transpose_x2(last)
            pe.wait_ge(dn_in, 16)
            for k in range(4):
                down(k, k, PAIR_STEPS[k][0])
                if k == 0:
                    routed_bias(0)
                    router(last)
                s = k + 2
                for ih in range(2):
                    gate_up(s, s % 4, ih, s // 4 * 2 + PAIR_STEPS[s % 4][0] + 1)
            with pe.Fori(1, PAIRS - 1) as i:
                for k in range(4):
                    down(i * 4 + k, k, i * 2 + PAIR_STEPS[k][0])
                    s = k + 2
                    for ih in range(2):
                        gate_up(i * 4 + s, s % 4, ih, i * 2 + s // 4 * 2 + PAIR_STEPS[s % 4][0] + 1)
            i = PAIRS - 1
            pe.wait_ge(logit_ready, BATCHES)
            transpose_weights(1)
            for k in range(4):
                down(i * 4 + k, k, i * 2 + PAIR_STEPS[k][0], tiles_apart=(k == 3))
                s = k + 2
                if s < 4:
                    for ih in range(2):
                        gate_up(i * 4 + s, s, ih, i * 2 + PAIR_STEPS[s][0] + 1)
                if k == 0:
                    routed_bias(1)


def kernel(x, ctx_1024, L0_xattn_Wq, L0_xattn_bq, L0_xattn_Wk, L0_xattn_bk, L0_xattn_Wv, L0_xattn_bv,
           L0_ffn_router_weight, L0_ffn_router_bias, L0_ffn_gate_up_proj, L0_ffn_gate_up_bias,
           L0_ffn_down_proj, L0_ffn_down_bias):
    import concourse.bacc as bacc
    from concourse.bass_utils import run_bass_kernel_spmd

    a = np.ascontiguousarray
    arrays = {
        "in_x": a(x), "in_ctx": a(ctx_1024),
        "in_att_w": a(np.concatenate([L0_xattn_Wq, np.asarray(L0_xattn_Wk).T, np.asarray(L0_xattn_bq)[:, None],
                                      np.asarray(L0_xattn_bk)[:, None]], axis=1)),
        "in_more_w": a(np.concatenate([L0_xattn_Wv, np.asarray(L0_ffn_router_weight).T,
                                       np.asarray(L0_ffn_gate_up_bias).reshape(EXPERTS * 4, P).T], axis=1)),
        "in_rows": a(np.concatenate([L0_xattn_bv, L0_ffn_router_bias])),
        "in_gu": a(L0_ffn_gate_up_proj), "in_dn": a(L0_ffn_down_proj), "in_db": a(L0_ffn_down_bias),
    }
    nc = bacc.Bacc("TRN2", target_bir_lowering=False, num_devices=1)
    args = [nc.dram_tensor(n, v.shape, mybir.dt.from_np(v.dtype), kind="ExternalInput").ap() for n, v in arrays.items()]
    out = nc.dram_tensor("out_x", (BATCHES, QUERIES, DIM), F32, kind="ExternalOutput").ap()
    build(nc, *args, out)
    r = run_bass_kernel_spmd(nc, [arrays], core_ids=[0])
    return r.results[0]["out_x"]
```
